# Optimizing a Trainium2 kernel written in Bass

```python
import numpy as np
import jax
import jax.numpy as jnp

def _softmax(x, axis=-1):
    return jax.nn.softmax(x, axis=axis)

def _gelu(x):
    return jax.nn.gelu(x, approximate=True)

def _silu(x):
    return jax.nn.silu(x)

def _sigmoid(x):
    return jax.nn.sigmoid(x)

def _layernorm(x, axis=-1, eps=1e-05):
    m = jnp.mean(x, axis=axis, keepdims=True)
    v = jnp.var(x, axis=axis, keepdims=True)
    return (x - m) / jnp.sqrt(v + eps)

def _scatter_add(tgt, idx, src, axis=0):
    return tgt.at[idx].add(src)

def _segment_sum(src, seg, n):
    return jax.ops.segment_sum(src, seg, n)
kernel_name = 'mk_early_fusion_d1_tok_img256_r4_c5a8d3'

def setup_inputs(seed: int=0):
    np.random.seed(seed)
    _w = jnp.asarray

    def _rec_inputs():
        import jax
        import jax.numpy as jnp
        _rk = jax.random.key(seed)
        x = -7.10856e-05 + 0.999911 * jax.random.normal(jax.random.fold_in(_rk, 1), (4, 64, 128, 64), jnp.float32)
        txt = -0.000161634 + 0.479995 * jax.random.normal(jax.random.fold_in(_rk, 2), (4, 128, 64), jnp.float32)
        return (x, txt)
    x, txt = _rec_inputs()

    def _L0_tok_setup():
        import jax, jax.numpy as jnp
        import numpy as np
        PATCH_LEN = 16
        STRIDE = 8
        PAD = 8
        key = jax.random.key(seed)
        k1, k2 = jax.random.split(key)
        x = jax.random.normal(k1, (32, 64, 128, 64), dtype=jnp.float32)
        in_feat = 64 * (PATCH_LEN // 2 + 1) * 2
        W = jax.random.normal(k2, (64, in_feat), dtype=jnp.float32) * 0.02
        return {'x': x, 'W': W}
    _L0_tok_all = _L0_tok_setup()
    _L0_tok_in = {k: v for k, v in _L0_tok_all.items() if k in ('W',)}
    del _L0_tok_all

    def _L0_attn_setup():
        import jax, jax.numpy as jnp
        import numpy as np
        D, N, K = (64, 64, 4)
        B, L = (2, 512)

        def _init_forget_gate(size, a=0.001, b=0.1, lo=-9.0, hi=-4.323):
            x = np.log(np.expm1(np.linspace(a, b, size, dtype=np.float64)))
            x = (x - x.min()) / (x.max() - x.min())
            return (x * abs(hi - lo) + lo).astype(np.float32)
        key = jax.random.key(seed)
        ks = jax.random.split(key, 7)
        x = jax.random.normal(ks[0], (B, L, D), jnp.float32)
        W_in = jax.random.normal(ks[1], (2 * D, D), jnp.float32) * D ** (-0.5)
        conv_w = jax.random.normal(ks[2], (D, 1, K), jnp.float32) * K ** (-0.5)
        conv_b = jax.random.normal(ks[3], (D,), jnp.float32) * 0.02
        W_bc = jax.random.normal(ks[4], (2 * N, D), jnp.float32) * N ** (-0.5)
        b_bc = jnp.zeros((2 * N,), jnp.float32)
        W_lam = jax.random.normal(ks[5], (D, D), jnp.float32) * D ** (-0.5)
        b_lam = jnp.zeros((D,), jnp.float32)
        A = jnp.tile(jnp.asarray(_init_forget_gate(D))[None, :], (N, 1))
        W_out = jax.random.normal(ks[6], (D, D), jnp.float32) * D ** (-0.5)
        return dict(x=x, W_in=W_in, conv_w=conv_w, conv_b=conv_b, W_bc=W_bc, b_bc=b_bc, W_lam=W_lam, b_lam=b_lam, A=A, W_out=W_out)
    _L0_attn_all = _L0_attn_setup()
    _L0_attn_in = {k: v for k, v in _L0_attn_all.items() if k in ('W_in', 'conv_w', 'conv_b', 'W_bc', 'b_bc', 'W_lam', 'b_lam', 'A', 'W_out')}
    del _L0_attn_all

    def _L0_ffn_setup():
        import jax, jax.numpy as jnp
        import numpy as np
        DIM = 64
        HEADS = 8
        NUM_KEYS = 64
        NUM_KV = NUM_KEYS ** 2
        PK_TOPK = 16
        FINAL_TOPK = 16
        DIM_KEY = DIM // 2
        P = 2

        def _pk(x, Wq_pk, pk_keys):
            b, n, _ = x.shape
            q = (x @ Wq_pk).reshape(b, n, P, HEADS, DIM_KEY).transpose(2, 0, 1, 3, 4)
            sim = jnp.einsum('pbnhd,pkhd->pbnhk', q, pk_keys)
            scores, idx = jax.lax.top_k(sim, PK_TOPK)
            idx0 = idx[0]
            idx1 = idx[1] * NUM_KEYS
            index = (idx0[..., :, None] + idx1[..., None, :]).reshape(b, n, HEADS, PK_TOPK * PK_TOPK)
            score = (scores[0][..., :, None] + scores[1][..., None, :]).reshape(b, n, HEADS, PK_TOPK * PK_TOPK)
            final_scores, pk_idx = jax.lax.top_k(score, FINAL_TOPK)
            final_indices = jnp.take_along_axis(index, pk_idx, axis=-1)
            final_scores = jax.nn.softmax(final_scores, axis=-1)
            return (final_scores, final_indices)
        key = jax.random.key(seed)
        ks = jax.random.split(key, 7)
        b, n = (2, 256)
        std = 0.02
        x = jax.random.normal(ks[0], (b, n, DIM), dtype=jnp.float32)
        Wq_pk = jax.random.normal(ks[1], (DIM, P * HEADS * DIM_KEY), dtype=jnp.float32) * std
        pk_keys = jax.random.normal(ks[2], (P, NUM_KEYS, HEADS, DIM_KEY), dtype=jnp.float32) * std
        Wq = jax.random.normal(ks[3], (DIM, HEADS * DIM), dtype=jnp.float32) * std
        keys_table = jax.random.normal(ks[4], (NUM_KV * HEADS, DIM), dtype=jnp.float32) * std
        values_table = jax.random.normal(ks[5], (NUM_KV * HEADS, DIM), dtype=jnp.float32) * std
        Wo = jax.random.normal(ks[6], (DIM * HEADS, DIM), dtype=jnp.float32) * std
        return {'x': x, 'Wq_pk': Wq_pk, 'pk_keys': pk_keys, 'Wq': Wq, 'keys_table': keys_table, 'values_table': values_table, 'Wo': Wo}
    _L0_ffn_all = _L0_ffn_setup()
    _L0_ffn_in = {k: v for k, v in _L0_ffn_all.items() if k in ('Wq_pk', 'pk_keys', 'Wq', 'keys_table', 'values_table', 'Wo')}
    del _L0_ffn_all
    return {'x': x, 'txt': txt, 'L0_tok_W': _L0_tok_in['W'], 'L0_attn_W_in': _L0_attn_in['W_in'], 'L0_attn_conv_w': _L0_attn_in['conv_w'], 'L0_attn_conv_b': _L0_attn_in['conv_b'], 'L0_attn_W_bc': _L0_attn_in['W_bc'], 'L0_attn_b_bc': _L0_attn_in['b_bc'], 'L0_attn_W_lam': _L0_attn_in['W_lam'], 'L0_attn_b_lam': _L0_attn_in['b_lam'], 'L0_attn_A': _L0_attn_in['A'], 'L0_attn_W_out': _L0_attn_in['W_out'], 'L0_ffn_Wq_pk': _L0_ffn_in['Wq_pk'], 'L0_ffn_pk_keys': _L0_ffn_in['pk_keys'], 'L0_ffn_Wq': _L0_ffn_in['Wq'], 'L0_ffn_keys_table': _L0_ffn_in['keys_table'], 'L0_ffn_values_table': _L0_ffn_in['values_table'], 'L0_ffn_Wo': _L0_ffn_in['Wo']}

def reference(x, txt, L0_tok_W, L0_attn_W_in, L0_attn_conv_w, L0_attn_conv_b, L0_attn_W_bc, L0_attn_b_bc, L0_attn_W_lam, L0_attn_b_lam, L0_attn_A, L0_attn_W_out, L0_ffn_Wq_pk, L0_ffn_pk_keys, L0_ffn_Wq, L0_ffn_keys_table, L0_ffn_values_table, L0_ffn_Wo):
    import jax
    import jax.numpy as jnp

    def _L0_tok_ref(x, W):
        import jax, jax.numpy as jnp
        import numpy as np
        PATCH_LEN = 16
        STRIDE = 8
        PAD = 8
        B, C, T, V = x.shape
        xp = jnp.pad(x, ((0, 0), (0, 0), (0, PAD), (0, 0)), mode='edge')
        Tp = T + PAD
        N = (Tp - PATCH_LEN) // STRIDE + 1
        idx = jnp.arange(N)[:, None] * STRIDE + jnp.arange(PATCH_LEN)[None, :]
        patches = xp[:, :, idx, :]
        patches = jnp.transpose(patches, (0, 4, 2, 3, 1))
        xf = jnp.fft.rfft(patches, axis=-2, norm='ortho')
        F = xf.shape[-2]
        x_real = xf.real.reshape(B, V, N, F * C)
        x_imag = xf.imag.reshape(B, V, N, F * C)
        x_emb = jnp.concatenate([x_real, x_imag], axis=-1)
        x_emb = x_emb @ W.T
        return x_emb.reshape(B, V * N, -1)

    def _L0_attn_ref(x, W_in, conv_w, conv_b, W_bc, b_bc, W_lam, b_lam, A, W_out):
        import jax, jax.numpy as jnp
        import numpy as np
        D, N, K = (64, 64, 4)
        B, L = (2, 512)

        def _init_forget_gate(size, a=0.001, b=0.1, lo=-9.0, hi=-4.323):
            x = np.log(np.expm1(np.linspace(a, b, size, dtype=np.float64)))
            x = (x - x.min()) / (x.max() - x.min())
            return (x * abs(hi - lo) + lo).astype(np.float32)
        Bb, Ll, d = x.shape
        n = A.shape[0]
        k = conv_w.shape[-1]
        proj = x @ W_in.T
        skip, u = (proj[..., :d], proj[..., d:])
        uc = jnp.transpose(u, (0, 2, 1))
        uc = jax.lax.conv_general_dilated(uc, conv_w, window_strides=(1,), padding=[(k - 1, 0)], dimension_numbers=('NCH', 'OIH', 'NCH'), feature_group_count=d)
        u = jnp.transpose(uc + conv_b[None, :, None], (0, 2, 1))
        bc = u @ W_bc.T + b_bc
        b, c = (bc[..., :n], bc[..., n:])
        lam = jnp.exp(jnp.einsum('bld,nd->blnd', jax.nn.sigmoid(u @ W_lam.T + b_lam), -8.0 * jax.nn.softplus(A)))
        bu = jnp.einsum('bln,bld->blnd', b, u) * jnp.sqrt(1.0 - lam ** 2 + 1e-06)

        def combine(e1, e2):
            a1, b1 = e1
            a2, b2 = e2
            return (a1 * a2, a2 * b1 + b2)
        _, h = jax.lax.associative_scan(combine, (lam, bu), axis=1)
        y = jnp.einsum('bln,blnd->bld', c, h)
        return jax.nn.gelu(skip, approximate=False) * y @ W_out.T

    def _L0_ffn_ref(x, Wq_pk, pk_keys, Wq, keys_table, values_table, Wo):
        import jax, jax.numpy as jnp
        import numpy as np
        DIM = 64
        HEADS = 8
        NUM_KEYS = 64
        NUM_KV = NUM_KEYS ** 2
        PK_TOPK = 16
        FINAL_TOPK = 16
        DIM_KEY = DIM // 2
        P = 2

        def _pk(x, Wq_pk, pk_keys):
            b, n, _ = x.shape
            q = (x @ Wq_pk).reshape(b, n, P, HEADS, DIM_KEY).transpose(2, 0, 1, 3, 4)
            sim = jnp.einsum('pbnhd,pkhd->pbnhk', q, pk_keys)
            scores, idx = jax.lax.top_k(sim, PK_TOPK)
            idx0 = idx[0]
            idx1 = idx[1] * NUM_KEYS
            index = (idx0[..., :, None] + idx1[..., None, :]).reshape(b, n, HEADS, PK_TOPK * PK_TOPK)
            score = (scores[0][..., :, None] + scores[1][..., None, :]).reshape(b, n, HEADS, PK_TOPK * PK_TOPK)
            final_scores, pk_idx = jax.lax.top_k(score, FINAL_TOPK)
            final_indices = jnp.take_along_axis(index, pk_idx, axis=-1)
            final_scores = jax.nn.softmax(final_scores, axis=-1)
            return (final_scores, final_indices)
        b, n, d = x.shape
        q = (x @ Wq).reshape(b, n, HEADS, DIM) * DIM ** (-0.5)
        kv_scores, indices = _pk(x, Wq_pk, pk_keys)
        offsets = jnp.arange(HEADS, dtype=indices.dtype) * NUM_KV
        ind = indices + offsets[None, None, :, None]
        k = jnp.einsum('bnhk,bnhkd->bnhd', kv_scores, keys_table[ind])
        v = jnp.einsum('bnhk,bnhkd->bnhd', kv_scores, values_table[ind])
        sim = jnp.einsum('bihd,bjhd->bhij', q, k)
        neg = -jnp.finfo(sim.dtype).max
        causal = jnp.tril(jnp.ones((n, n), dtype=bool))
        sim = jnp.where(causal, sim, neg)
        attn = jax.nn.softmax(sim, axis=-1)
        out = jnp.einsum('bhij,bjhd->bhid', attn, v)
        out = out.transpose(0, 2, 1, 3).reshape(b, n, HEADS * DIM)
        return out @ Wo
    h = _L0_tok_ref(x, L0_tok_W)
    h = jnp.concatenate([h, txt], axis=1)
    h = h + _L0_attn_ref(_layernorm(h, axis=-1), L0_attn_W_in, L0_attn_conv_w, L0_attn_conv_b, L0_attn_W_bc, L0_attn_b_bc, L0_attn_W_lam, L0_attn_b_lam, L0_attn_A, L0_attn_W_out)
    h = h + _L0_ffn_ref(_layernorm(h, axis=-1), L0_ffn_Wq_pk, L0_ffn_pk_keys, L0_ffn_Wq, L0_ffn_keys_table, L0_ffn_values_table, L0_ffn_Wo)
    return h

_drawn_inputs = setup_inputs


def setup_inputs(seed=0):
    import zlib

    import numpy as np

    out = dict(_drawn_inputs(seed))
    spreads = {'L0_attn_b_bc': (0.0, 0.1), 'L0_attn_b_lam': (0.0, 0.417)}
    factors = {'L0_ffn_Wq_pk': 64.0,
     'L0_ffn_pk_keys': 64.0,
     'L0_ffn_Wq': 64.0,
     'L0_ffn_keys_table': 64.0,
     'L0_ffn_values_table': 64.0,
     'L0_ffn_Wo': 64.0}
    for name, (base, spread) in spreads.items():
        noise = np.random.default_rng([zlib.crc32(name.encode()), seed]).standard_normal(out[name].shape)
        drawn = base * np.exp(spread * noise) if base else spread * noise
        out[name] = jnp.asarray(drawn.astype(out[name].dtype))
    for name, factor in factors.items():
        out[name] = (out[name] * factor).astype(out[name].dtype)
    return out
```

```python
from contextlib import ExitStack

import numpy as np

import concourse.bass as bass
from concourse import mybir

F32 = mybir.dt.float32
U32 = mybir.dt.uint32
ALU = mybir.AluOpType
ACT = mybir.ActivationFunctionType
AX = mybir.AxisListType

P = 128
BATCH, CHANNELS, TIME, VARS = 4, 64, 128, 64
PATCH, STRIDE = 16, 8
PATCHES = TIME // STRIDE
FREQS = PATCH // 2 + 1
DIM = 64
TEXT = 128
TOKENS = VARS * PATCHES
LEN = TOKENS + TEXT
TILES = LEN // P
STATE = 64
TAPS = 4
PAIRS = STATE // 2
CHUNKS = 3
CH = LEN // CHUNKS
UNITS = CHUNKS * PAIRS
GROUP = 4
HEADS = 8
KEYS = 64
TOP = 16
KEYDIM = 32
ROW = 2 * DIM
LIMITS = [TOP // (a + 1) for a in range(TOP)]
PLACES = [sum(LIMITS[:a]) for a in range(TOP)]
CANDS = sum(LIMITS)
LOWEST = float(np.finfo(np.float32).min)
MASKED = -1e30
LN_EPS = 1e-5
DECAY_EPS = 1e-6
RANK_STEPS = 25


def stages(kind):
    if kind == "first":
        yield "front", 0, 0
        for c in range(CHUNKS):
            yield "units", c * PAIRS, PAIRS
            yield "chunk", c, 0
        yield "norm", 0, 0
        yield "rank", 0, 0
        return
    ahead = kind == "turn"
    for t in range(TILES):
        yield "query", t, 0
        if ahead and t == TILES - 1:
            yield "norm", 0, 0
        if ahead or t + 1 < TILES:
            yield "rank", t + 1, 0
        if ahead and t == 0:
            yield "front", 0, 0
        for hp in range(HEADS // 2):
            if ahead and t < TILES - 1 and hp < 3:
                u = (3 * t + hp) * GROUP
                yield "units", u, GROUP
                if (u + GROUP) % PAIRS == 0:
                    yield "chunk", u // PAIRS, 0
            yield "heads", t, hp
        yield "finish", t, 0


def wide_steps(kind):
    out = ["weff", "wcomb"] if kind == "first" else []
    for name, a, hp in stages(kind):
        if name == "front":
            out += ["tok0", "tok1", "mean1", "var1", "skip", "u", "bc", "lam"]
        elif name == "norm":
            out += ["mean2", "var2"]
        elif name == "rank":
            out += [("sim", a)]
        elif name == "heads":
            out += [(s, a, h) for h in (2 * hp, 2 * hp + 1) for s in ("score", "turned")]
    return out


def small_steps(kind, filled):
    out = []
    for name, a, hp in stages(kind):
        if name == "query":
            out += [("q", a), ("res", a)]
        elif name == "chunk":
            out += [("out", a)]
        elif name == "heads":
            out += [] if filled else [("kv", a, 2 * hp), ("kv", a, 2 * hp + 1)]
            out += [("keys", a, hp)]
    return out


class Count:

    def __init__(self, sem, lists):
        self.sem = sem
        self.at = {kind: {key: i for i, key in enumerate(steps)} for kind, steps in lists.items()}
        self.first, self.turn = len(lists["first"]), len(lists["turn"])

    def before(self, kind, b, key):
        i = self.at[kind][key]
        return i if kind == "first" else b * self.turn + (self.first + i)

    def after(self, kind, b, key):
        i = self.at[kind][key] + 1
        return i if kind == "first" else b * self.turn + (self.first + i)


def program(nc, x, text, text_t, w_tok, dft, w_in, conv_w, conv_b, w_bc, b_bc, w_lam, b_lam, decay, w_out,
            w_qpk, keys, w_q, tables, w_o, ident_d, fold_d, causal_d, out):
    kinds = ("first", "turn", "last")
    with ExitStack() as ctx:
        def sb(name, shape, dt=F32):
            return ctx.enter_context(nc.sbuf_tensor(name, shape, dt))

        def ps(name, shape):
            return ctx.enter_context(nc.psum_tensor(name, shape, F32))

        def sem(name):
            return ctx.enter_context(nc.semaphore(name))

        wide = ps("wide", [P, 3, 512])
        small = ps("small", [P, 512])
        attn = ps("attn", [P, 512])
        bwide = ps("bwide", [P, 512])
        cwide = ps("cwide", [P, 512])
        ysum = ps("ysum", [P, 512])
        wide_flat = wide[:].rearrange("p a b -> p (a b)")

        ident = sb("ident", [P, P])
        fold = sb("fold", [P, DIM])
        causal = sb("causal", [P, P])
        dft_s = sb("dft_s", [2 * FREQS, PATCH])
        mean_w = sb("mean_w", [DIM, DIM])
        one_eps = sb("one_eps", [P, 1])
        ln_eps = sb("ln_eps", [P, 1])
        w_eff = sb("w_eff", [P, STRIDE, DIM])
        win = sb("win", [DIM, 3, DIM])
        cw = sb("cw", [P, TAPS])
        cb = sb("cb", [P, 1])
        wbc = sb("wbc", [DIM, P])
        bbc = sb("bbc", [P, 1])
        wlam = sb("wlam", [DIM, 2, DIM])
        blam = sb("blam", [P, 1])
        nblam = sb("nblam", [P, 1])
        wout = sb("wout", [DIM, DIM])
        raw_a = sb("raw_a", [P, PAIRS])
        coef = sb("coef", [P, PAIRS])
        coef2 = sb("coef2", [P, PAIRS])
        sp = [sb(f"sp{i}", [P, PAIRS]) for i in range(4)]
        wcomb = sb("wcomb", [DIM, 2 * HEADS * KEYS])
        wq = sb("wq", [DIM, HEADS * DIM])
        wo = sb("wo", [P, HEADS * DIM // P, DIM])
        head_base = sb("head_base", [P, HEADS, TOP], U32)
        place = sb("place", [P, CANDS], U32)

        h_t = sb("h_t", [DIM, LEN])
        upad = sb("upad", [P, LEN + TAPS - 1])
        x_c = upad[0:DIM, TAPS - 1:]
        bc_t = sb("bc_t", [P, LEN])
        sq = bc_t[0:DIM, :]
        inv = bc_t[0:DIM, :]
        u_t = sb("u_t", [P, LEN])
        rr = u_t[0:DIM, :]
        sig = sb("sig", [P, LEN])
        gate = sb("gate", [DIM, LEN])
        h1_t = sb("h1_t", [DIM, LEN])
        xn_t = sb("xn_t", [DIM, LEN])
        carry = sb("carry", [P, PAIRS])
        gy = sb("gy", [DIM, CH])
        arena = sb("arena", [P, 12 * CH])
        x2 = arena[:, 0:64 * VARS].rearrange("p (t v) -> p t v", v=VARS)

        def ring(first, n):
            return [arena[:, (first + i) * CH:(first + i + 1) * CH] for i in range(n)]

        lam_r, v_r, z_r, hs_r, cy_r = ring(0, 3), ring(3, 3), ring(6, 2), ring(8, 2), ring(10, 2)

        sims = sb("sims", [P, 2 * HEADS, KEYS])
        top_v = sb("top_v", [P, 2 * HEADS, TOP])
        top_i = sb("top_i", [P, 2 * HEADS, TOP], U32)
        idx1 = sb("idx1", [P, HEADS, TOP])
        cand = sb("cand", [P, HEADS, CANDS])
        cand_i = sb("cand_i", [P, HEADS, CANDS])
        best = sb("best", [P, HEADS, TOP])
        best_at = sb("best_at", [P, HEADS, TOP], U32)
        hot = sb("hot", [P, 2, TOP, CANDS])
        row_f = sb("row_f", [P, HEADS, TOP])
        expo = sb("expo", [P, HEADS, TOP])
        zsum = sb("zsum", [P, HEADS])
        zinv = sb("zinv", [P, HEADS])
        row_i = sb("row_i", [P, 3, HEADS * TOP], U32)
        weight = sb("weight", [P, 3, HEADS, TOP])

        rows = sb("rows", [P, HEADS, TOP, ROW])
        vals = sb("vals", [P, TILES, HEADS, DIM])
        k_nat = sb("k_nat", [P, 2, DIM])
        k_t = sb("k_t", [P, HEADS // 2, LEN])
        q_t = sb("q_t", [P, HEADS // 2, P])
        res = sb("res", [P, DIM])
        nmax = sb("nmax", [P, HEADS])
        rsum = sb("rsum", [P, HEADS])
        rinv = sb("rinv", [P, HEADS])
        prob = sb("prob", [P, LEN])
        prob_t = sb("prob_t", [P, LEN])
        o_n = sb("o_n", [P, HEADS, DIM])
        o_t = sb("o_t", [P, HEADS * DIM // P, P])
        out_s = sb("out_s", [P, DIM])

        rows_flat = rows[:].rearrange("p h j r -> p (h j r)")
        w18 = rows_flat[0:2 * FREQS, 0:DIM * CHANNELS].rearrange("r (o c) -> r o c", o=DIM)
        wqpk_s = rows_flat[0:KEYDIM, 4096:5120].rearrange("d (g i) -> d g i", i=DIM)
        keys_s = rows_flat[0:KEYDIM, 5120:6144].rearrange("d (g k) -> d g k", k=KEYS)

        weights_in = sem("weights_in")
        passed = sem("passed")
        set_up = sem("set_up")
        spread = sem("spread")
        pos_ready = sem("pos_ready")
        x_in = [sem("x_in0"), sem("x_in1")]
        text_in = sem("text_in")
        wide_filled = Count(sem("wide_filled"), {k: wide_steps(k) for k in kinds})
        wide_drained = Count(sem("wide_drained"), {k: wide_steps(k) for k in kinds})
        small_filled = Count(sem("small_filled"), {k: small_steps(k, True) for k in kinds})
        small_drained = Count(sem("small_drained"), {k: small_steps(k, False) for k in kinds})
        centred = sem("centred")
        squared = sem("squared")
        log_ready = sem("log_ready")
        inv_ready = sem("inv_ready")
        newton = sem("newton")
        normed = sem("normed")
        convolved = sem("convolved")
        sig_step = sem("sig_step")
        lam_ready = sem("lam_ready")
        lam2_ready = sem("lam2_ready")
        z_log = sem("z_log")
        z_ready = sem("z_ready")
        b_ready = sem("b_ready")
        c_ready = sem("c_ready")
        bu_ready = sem("bu_ready")
        scaled = sem("scaled")
        scanned = sem("scanned")
        carried = sem("carried")
        cy_ready = sem("cy_ready")
        y_summed = sem("y_summed")
        gated = sem("gated")
        h1_copied = sem("h1_copied")
        rank_step = sem("rank_step")
        shifted = sem("shifted")
        expo_ready = sem("expo_ready")
        row_i_ready = sem("row_i_ready")
        weight_ready = sem("weight_ready")
        gathered = [sem(f"gathered{h}") for h in range(HEADS)]
        weighted = sem("weighted")
        rows_summed = [sem(f"rows_summed{h}") for h in range(HEADS)]
        max_ready = sem("max_ready")
        o_filled = sem("o_filled")
        o_inv = sem("o_inv")
        o_normed = sem("o_normed")
        o_turned = sem("o_turned")
        o_t_ready = sem("o_t_ready")
        fin_filled = sem("fin_filled")
        out_ready = sem("out_ready")
        stored = sem("stored")

        loads = [
            (ident[:], ident_d), (fold[:], fold_d), (causal[:], causal_d), (dft_s[:], dft),
            (w18, w_tok), (wqpk_s, w_qpk), (keys_s, keys),
            (win[:, 0, :], w_in[:, 0:DIM]), (win[:, 1, :], w_in[:, DIM:]), (win[:, 2, :], w_in[:, DIM:]),
            (cw[0:DIM, :], conv_w), (cw[DIM:P, :], conv_w), (cb[0:DIM, :], conv_b), (cb[DIM:P, :], conv_b),
            (wbc[:], w_bc), (bbc[:], b_bc), (wlam[:, 0, :], w_lam), (wlam[:, 1, :], w_lam),
            (blam[0:DIM, :], b_lam), (blam[DIM:P, :], b_lam), (wout[:], w_out), (raw_a[:], decay),
            (wq[:], w_q), (wo[:], w_o),
        ]

        def ring_free(eng, s, value):
            if not isinstance(value, int) or value > 0:
                eng.wait_ge(s, value)

        def plain(eng):
            eng.sem_inc(passed, 1)

        def wide_view(parts):
            return wide[0:parts, :, 0:CH]

        def in_chunks(ap):
            return ap.rearrange("p (c k) -> p c k", c=CHUNKS)

        block = ctx.enter_context(nc.Block())

        @block.sync
        def _(sync):
            for dst, src in loads:
                sync.dma_start(dst, src).then_inc(weights_in, 16)

            def load_batch(kind, b, i):
                for half in range(2):
                    if half:
                        sync.wait_ge(wide_filled.sem, wide_filled.after(kind, b, "tok0"))
                    else:
                        ring_free(sync, y_summed, UNITS * i)
                    lo = 64 * half
                    sync.dma_start(x2[0:CHANNELS, :, :], x[i, :, lo:lo + 64, :]).then_inc(x_in[half], 16)
                    if half == 0:
                        sync.dma_start(x2[CHANNELS:P, :, :],
                                       x[i, :, STRIDE:STRIDE + 64, :]).then_inc(x_in[0], 16)
                        ring_free(sync, h1_copied, i)
                        sync.dma_start(h_t[:, TOKENS:LEN], text_t[i]).then_inc(text_in, 16)
                    else:
                        last = 64 - STRIDE
                        sync.dma_start(x2[CHANNELS:P, 0:last, :],
                                       x[i, :, lo + STRIDE:TIME, :]).then_inc(x_in[1], 16)
                        sync.dma_start(x2[CHANNELS:P, last:64, :],
                                       x[i, :, TIME - 1:TIME, :].broadcast_to([CHANNELS, STRIDE, VARS])
                                       ).then_inc(x_in[1], 16)

            def store(b, t):
                sync.wait_ge(out_ready, TILES * b + t + 1)
                sync.dma_start(out[b, t * P:(t + 1) * P, :], out_s[:]).then_inc(stored, 16)

            load_batch("first", 0, 0)
            with sync.Fori(0, BATCH - 1) as b:
                load_batch("turn", b, b + 1)
                for t in range(TILES):
                    store(b, t)
            for t in range(TILES):
                store(BATCH - 1, t)
            sync.wait_ge(stored, 16 * TILES * BATCH)

        @block.gpsimd
        def _(pool):
            nc.gpsimd.iota(head_base[:], [[KEYS * KEYS, HEADS], [0, TOP]], base=0,
                           channel_multiplier=0).then_inc(pos_ready, 1)
            nc.gpsimd.iota(place[:], [[1, CANDS]], base=0, channel_multiplier=0).then_inc(pos_ready, 1)
            pool.wait_ge(wide_filled.sem, wide_filled.after("first", 0, "wcomb"))

            def gather(b):
                for t in range(TILES):
                    g = TILES * b + t
                    pool.wait_ge(row_i_ready, g + 1)
                    for h in range(HEADS):
                        pool.wait_ge(rows_summed[h], g)
                        plain(pool)
                        for j in range(TOP):
                            at = h * TOP + j
                            nc.gpsimd.indirect_dma_start(
                                rows[:, h, j, :], None, tables,
                                bass.IndirectOffsetOnAxis(ap=row_i[:, t % 3, at:at + 1], axis=0),
                            ).then_inc(gathered[h], 16)

            with pool.Fori(0, BATCH - 1) as b:
                gather(b)
            gather(BATCH - 1)

        @block.scalar
        def _(act):
            nc.scalar.preload_act_table_set(EXP_AND_LN)
            act.wait_ge(weights_in, 16 * len(loads))
            act.wait_ge(wide_filled.sem, wide_filled.after("first", 0, "weff"))
            nc.scalar.copy(w_eff[:].rearrange("p k o -> p (k o)"), wide_flat[:, 0:512]).then_inc(wide_drained.sem, 1)
            act.wait_ge(wide_filled.sem, wide_filled.after("first", 0, "wcomb"))
            nc.scalar.copy(wcomb[:], wide_flat[0:DIM, 0:1024]).then_inc(wide_drained.sem, 1)
            act.wait_ge(set_up, 2)
            nc.scalar.activation(sp[1][:], sp[0][:], ACT.Exp).then_inc(spread, 1)
            act.wait_ge(set_up, SETUP_STEPS)

            def full(kind, b, key):
                act.wait_ge(wide_filled.sem, wide_filled.after(kind, b, key))

            def inverse_root(kind, b, n, which):
                full(kind, b, f"var{which}")
                nc.scalar.activation(in_chunks(inv), wide_view(DIM), ACT.Ln, bias=ln_eps[0:DIM, :]
                                     ).then_inc(log_ready, 1)
                act.wait_ge(log_ready, n + 1)
                nc.scalar.activation(inv, inv, ACT.Exp, scale=-0.5).then_inc(inv_ready, 1)

            def front(kind, b, i):
                for half in range(2):
                    full(kind, b, f"tok{half}")
                    if half == 0:
                        ring_free(act, h1_copied, i)
                    dst = h_t[:, 0:TOKENS].rearrange("o (v n) -> o n v", n=PATCHES)[:, 8 * half:8 * half + 8, :]
                    src = wide[0:DIM, 0, :].rearrange("o (n v) -> o n v", v=VARS)
                    nc.scalar.copy(dst, src).then_inc(wide_drained.sem, 1)
                inverse_root(kind, b, 2 * i, 1)
                full(kind, b, "skip")
                nc.scalar.activation(in_chunks(gate[:]), wide_view(DIM), ACT.Gelu).then_inc(wide_drained.sem, 1)
                nc.scalar.preload_act_table_set(EXP_AND_LN)
                full(kind, b, "u")
                nc.scalar.copy(in_chunks(upad[:, TAPS - 1:]), wide_view(P)).then_inc(wide_drained.sem, 1)
                full(kind, b, "bc")
                nc.scalar.activation(in_chunks(bc_t[:]), wide_view(P), ACT.Identity, bias=bbc[:]
                                     ).then_inc(wide_drained.sem, 1)
                full(kind, b, "lam")
                nc.scalar.activation(in_chunks(sig[:]), wide_view(P), ACT.Exp, bias=nblam[:], scale=-1.0
                                     ).then_inc(wide_drained.sem, 1)

            def units(i, u0, n):
                for u in range(u0, u0 + n):
                    c, p = divmod(u, PAIRS)
                    done = UNITS * i + u
                    s = sig[:, c * CH:(c + 1) * CH]
                    if u == u0:
                        act.wait_ge(sig_step, 2 * i + 2)
                    ring_free(act, scanned, done - 2)
                    nc.scalar.activation(lam_r[u % 3], s, ACT.Exp, scale=coef[:, p:p + 1]).then_inc(lam_ready, 1)
                    ring_free(act, scaled, done - 1)
                    nc.scalar.activation(z_r[u % 2], s, ACT.Exp, scale=coef2[:, p:p + 1]).then_inc(lam2_ready, 1)
                    act.wait_ge(lam2_ready, done + 1)
                    nc.scalar.activation(z_r[u % 2], z_r[u % 2], ACT.Ln, bias=one_eps[:], scale=-1.0
                                         ).then_inc(z_log, 1)
                    act.wait_ge(z_log, done + 1)
                    nc.scalar.activation(z_r[u % 2], z_r[u % 2], ACT.Exp, scale=0.5).then_inc(z_ready, 1)

            def norm(kind, b, i):
                inverse_root(kind, b, 2 * i + 1, 2)
                act.wait_ge(normed, 2 * i + 2)
                nc.scalar.copy(h1_t[:], h_t[:]).then_inc(h1_copied, 1)

            def query(kind, b, t):
                act.wait_ge(small_filled.sem, small_filled.after(kind, b, ("q", t)))
                nc.scalar.mul(q_t[:].rearrange("p a t -> p (a t)"), small[:], DIM ** -0.5
                              ).then_inc(small_drained.sem, 1)
                act.wait_ge(small_filled.sem, small_filled.after(kind, b, ("res", t)))
                act.wait_ge(out_ready, TILES * b + t)
                nc.scalar.copy(res[:], small[:, 0:DIM]).then_inc(small_drained.sem, 1)

            def rank(kind, b, t, g):
                full(kind, b, ("sim", t))
                ring_free(act, rank_step, RANK_STEPS * g)
                nc.scalar.copy(sims[:].rearrange("p g k -> p (g k)"), wide_flat[:, 0:1024]
                               ).then_inc(wide_drained.sem, 1)
                act.wait_ge(shifted, g + 1)
                ring_free(act, weight_ready, g)
                nc.scalar.activation(expo[:], best[:], ACT.Exp).then_inc(expo_ready, 1)

            def heads(kind, b, t, hp):
                g = TILES * b + t
                n = (t + 1) * P
                for h in (2 * hp, 2 * hp + 1):
                    act.wait_ge(rows_summed[h], g + 1)
                    nc.scalar.copy(vals[:, t, h, :], small[:, DIM:ROW])
                    nc.scalar.copy(k_nat[:, h % 2, :], small[:, 0:DIM]).then_inc(small_drained.sem, 1)
                act.wait_ge(small_filled.sem, small_filled.after(kind, b, ("keys", t, hp)))
                nc.scalar.copy(k_t[:, hp, t * P:n], small[:, 0:P]).then_inc(small_drained.sem, 1)
                for h in (2 * hp, 2 * hp + 1):
                    act.wait_ge(max_ready, HEADS * g + h + 1)
                    nc.scalar.activation(prob[:, 0:n], wide_flat[:, 0:n], ACT.Exp, bias=nmax[:, h:h + 1],
                                         accum_out=rsum[:, h:h + 1]).then_inc(wide_drained.sem, 1)
                    full(kind, b, ("turned", t, h))
                    nc.scalar.copy(prob_t[:, 0:n], wide_flat[:, 0:n]).then_inc(wide_drained.sem, 1)

            def finish(g):
                act.wait_ge(o_turned, g + 1)
                nc.scalar.copy(o_t[:].rearrange("p c t -> p (c t)"), attn[:]).then_inc(o_t_ready, 1)

            def turn(kind, b):
                i = 0 if kind == "first" else b + 1
                for name, a, n in stages(kind):
                    if name == "front":
                        front(kind, b, i)
                    elif name == "units":
                        units(i, a, n)
                    elif name == "norm":
                        norm(kind, b, i)
                    elif name == "query":
                        query(kind, b, a)
                    elif name == "rank":
                        rank(kind, b, a, TILES * b + a)
                    elif name == "heads":
                        heads(kind, b, a, n)
                    elif name == "finish":
                        finish(TILES * b + a)

            turn("first", 0)
            with act.Fori(0, BATCH - 1) as b:
                turn("turn", b)
            turn("last", BATCH - 1)

        @block.vector
        def _(dve):
            nc.vector.memset(mean_w[:], 1.0 / DIM)
            nc.vector.memset(upad[:, 0:TAPS - 1], 0.0)
            nc.vector.memset(one_eps[:], 1.0 + DECAY_EPS)
            nc.vector.memset(ln_eps[:], LN_EPS)
            dve.wait_ge(weights_in, 16 * len(loads))
            count = [0]

            def step(ins):
                count[0] += 1
                ins.then_inc(set_up, 1)
                dve.wait_ge(set_up, count[0])

            step(nc.vector.tensor_scalar(sp[0][:], raw_a[:], -1.0, None, ALU.mult))
            step(nc.vector.tensor_tensor(sp[0][:], sp[0][:], raw_a[:], ALU.min))
            dve.wait_ge(spread, 1)
            step(nc.vector.tensor_scalar(sp[2][:], sp[1][:], 2.0, None, ALU.add))
            step(nc.vector.reciprocal(sp[2][:], sp[2][:]))
            step(nc.vector.tensor_tensor(sp[1][:], sp[1][:], sp[2][:], ALU.mult))
            step(nc.vector.tensor_tensor(sp[2][:], sp[1][:], sp[1][:], ALU.mult))
            step(nc.vector.tensor_scalar(sp[3][:], sp[2][:], 1.0 / SERIES[0], None, ALU.mult))
            for k in SERIES[1:]:
                step(nc.vector.scalar_tensor_tensor(sp[3][:], sp[3][:], 1.0 / k, sp[2][:], ALU.add, ALU.mult))
            step(nc.vector.scalar_tensor_tensor(sp[3][:], sp[3][:], 1.0, sp[1][:], ALU.add, ALU.mult))
            step(nc.vector.tensor_scalar(sp[0][:], raw_a[:], 0.0, None, ALU.max))
            step(nc.vector.scalar_tensor_tensor(sp[3][:], sp[3][:], 2.0, sp[0][:], ALU.mult, ALU.add))
            step(nc.vector.tensor_scalar(coef[:], sp[3][:], -8.0, None, ALU.mult))
            step(nc.vector.tensor_scalar(coef2[:], sp[3][:], -16.0, None, ALU.mult))
            step(nc.vector.tensor_scalar(nblam[:], blam[:], -1.0, None, ALU.mult))
            assert count[0] == SETUP_STEPS
            dve.wait_ge(pos_ready, 2)

            def full(kind, b, key):
                dve.wait_ge(wide_filled.sem, wide_filled.after(kind, b, key))

            def layer_norm(kind, b, n, which, dst):
                full(kind, b, f"mean{which}")
                ring_free(dve, normed, n)
                nc.vector.tensor_tensor(in_chunks(x_c), in_chunks(h_t[:]), wide_view(DIM), ALU.subtract
                                        ).then_inc(wide_drained.sem, 1)
                dve.wait_ge(wide_drained.sem, wide_drained.after(kind, b, f"mean{which}"))
                nc.vector.tensor_tensor(sq, x_c, x_c, ALU.mult).then_inc(squared, 1)
                full(kind, b, f"var{which}")
                dve.wait_ge(inv_ready, n + 1)
                nc.vector.tensor_tensor(rr, inv, inv, ALU.mult).then_inc(newton, 1)
                dve.wait_ge(newton, 3 * n + 1)
                nc.vector.scalar_tensor_tensor(in_chunks(rr), wide_view(DIM), LN_EPS, in_chunks(rr),
                                               ALU.add, ALU.mult).then_inc(wide_drained.sem, 1)
                dve.wait_ge(wide_drained.sem, wide_drained.after(kind, b, f"var{which}"))
                nc.vector.tensor_scalar(rr, rr, -0.5, 1.5, ALU.mult, ALU.add).then_inc(newton, 1)
                dve.wait_ge(newton, 3 * n + 2)
                nc.vector.tensor_tensor(rr, rr, inv, ALU.mult).then_inc(newton, 1)
                dve.wait_ge(newton, 3 * n + 3)
                nc.vector.tensor_tensor(dst, x_c, rr, ALU.mult).then_inc(normed, 1)

            def front(kind, b, i):
                dve.wait_ge(text_in, 16 * (i + 1))
                layer_norm(kind, b, 2 * i, 1, x_c)
                dve.wait_ge(wide_drained.sem, wide_drained.after(kind, b, "u"))
                nc.vector.tensor_scalar(u_t[:], upad[:, 0:LEN], cw[:, 0:1], cb[:, 0:1], ALU.mult, ALU.add
                                        ).then_inc(convolved, 1)
                for k in range(1, TAPS):
                    dve.wait_ge(convolved, TAPS * i + k)
                    nc.vector.scalar_tensor_tensor(u_t[:], upad[:, k:k + LEN], cw[:, k:k + 1], u_t[:],
                                                   ALU.mult, ALU.add).then_inc(convolved, 1)
                dve.wait_ge(wide_drained.sem, wide_drained.after(kind, b, "lam"))
                nc.vector.tensor_scalar(sig[:], sig[:], 1.0, None, ALU.add).then_inc(sig_step, 1)
                dve.wait_ge(sig_step, 2 * i + 1)
                nc.vector.reciprocal(sig[:], sig[:]).then_inc(sig_step, 1)
                dve.wait_ge(convolved, TAPS * i + TAPS)

            def units(i, u0, n):
                for s in range(u0, u0 + n + 3):
                    if s < u0 + n:
                        c = s // PAIRS
                        done = UNITS * i + s
                        dve.wait_ge(b_ready, done + 1)
                        ring_free(dve, scanned, done - 2)
                        nc.vector.tensor_tensor(v_r[s % 3], bwide[:, 0:CH], u_t[:, c * CH:(c + 1) * CH],
                                                ALU.mult).then_inc(bu_ready, 1)
                    if u0 <= s - 1 < u0 + n:
                        u = s - 1
                        done = UNITS * i + u
                        dve.wait_ge(bu_ready, done + 1)
                        dve.wait_ge(z_ready, done + 1)
                        v = v_r[u % 3]
                        nc.vector.tensor_tensor(v, z_r[u % 2], v, ALU.mult).then_inc(scaled, 1)
                    if u0 <= s - 2 < u0 + n:
                        u = s - 2
                        c, p = divmod(u, PAIRS)
                        done = UNITS * i + u
                        dve.wait_ge(scaled, done + 1)
                        dve.wait_ge(lam_ready, done + 1)
                        start = 0.0
                        if c:
                            start = carry[:, p:p + 1]
                            dve.wait_ge(carried, UNITS * i + u - PAIRS + 1)
                        ring_free(dve, cy_ready, done - 1)
                        nc.vector.tensor_tensor_scan(hs_r[u % 2], lam_r[u % 3], v_r[u % 3], start,
                                                     ALU.mult, ALU.add).then_inc(scanned, 1)
                    if u0 <= s - 3:
                        u = s - 3
                        p = u % PAIRS
                        done = UNITS * i + u
                        dve.wait_ge(scanned, done + 1)
                        nc.vector.tensor_copy(carry[:, p:p + 1], hs_r[u % 2][:, CH - 1:CH]).then_inc(carried, 1)
                        dve.wait_ge(c_ready, done + 1)
                        ring_free(dve, y_summed, done - 1)
                        nc.vector.tensor_tensor(cy_r[u % 2], hs_r[u % 2], cwide[:, 0:CH], ALU.mult
                                                ).then_inc(cy_ready, 1)

            def chunk(kind, b, i, c):
                dve.wait_ge(y_summed, UNITS * i + (c + 1) * PAIRS)
                cols = slice(c * CH, (c + 1) * CH)
                nc.vector.tensor_tensor(gy[:], gate[:, cols], ysum[0:DIM, 0:CH], ALU.mult).then_inc(gated, 1)
                dve.wait_ge(small_filled.sem, small_filled.after(kind, b, ("out", c)))
                nc.vector.tensor_tensor(h_t[:, cols], h_t[:, cols], small[0:DIM, 0:CH], ALU.add
                                        ).then_inc(small_drained.sem, 1)

            def rank(kind, b, t, g):
                base = RANK_STEPS * g
                count = [0]

                def after(ins):
                    count[0] += 1
                    ins.then_inc(rank_step, 1)
                    dve.wait_ge(rank_step, base + count[0])
                    plain(dve)

                dve.wait_ge(wide_drained.sem, wide_drained.after(kind, b, ("sim", t)))
                plain(dve)
                groups = range(2 * HEADS)
                for q in groups:
                    last = nc.vector.max(top_v[:, q, 0:8], sims[:, q, :])
                after(last)
                for q in groups:
                    nc.vector.max_index(top_i[:, q, 0:8], top_v[:, q, 0:8], sims[:, q, :])
                for q in groups:
                    last = nc.vector.match_replace(sims[:, q, :], top_v[:, q, 0:8], sims[:, q, :], LOWEST)
                after(last)
                for q in groups:
                    last = nc.vector.max(top_v[:, q, 8:16], sims[:, q, :])
                after(last)
                for q in groups:
                    last = nc.vector.max_index(top_i[:, q, 8:16], top_v[:, q, 8:16], sims[:, q, :])
                after(last)
                after(nc.vector.tensor_scalar(idx1[:], top_i[:, HEADS:, :], float(KEYS), None, ALU.mult))

                def pairs(dst, first, second):
                    for a in range(5):
                        m, o = LIMITS[a], PLACES[a]
                        nc.vector.tensor_tensor(dst[:, :, o:o + m], second[:, :, 0:m],
                                                first[:, :, a:a + 1].broadcast_to([P, HEADS, m]), ALU.add)
                    o = PLACES[5]
                    nc.vector.tensor_tensor(
                        dst[:, :, o:o + 6].rearrange("p h (a c) -> p h a c", c=2),
                        second[:, :, 0:2].unsqueeze(2).broadcast_to([P, HEADS, 3, 2]),
                        first[:, :, 5:8].unsqueeze(3).broadcast_to([P, HEADS, 3, 2]), ALU.add)
                    return nc.vector.tensor_tensor(dst[:, :, PLACES[8]:], first[:, :, 8:],
                                                   second[:, :, 0:1].broadcast_to([P, HEADS, 8]), ALU.add)

                pairs(cand[:], top_v[:, 0:HEADS, :], top_v[:, HEADS:, :])
                after(pairs(cand_i[:], top_i[:, 0:HEADS, :], idx1[:]))
                for h in range(HEADS):
                    last = nc.vector.max(best[:, h, 0:8], cand[:, h, :])
                after(last)
                for h in range(HEADS):
                    nc.vector.max_index(best_at[:, h, 0:8], best[:, h, 0:8], cand[:, h, :])
                for h in range(HEADS):
                    last = nc.vector.match_replace(cand[:, h, :], best[:, h, 0:8], cand[:, h, :], LOWEST)
                after(last)
                for h in range(HEADS):
                    last = nc.vector.max(best[:, h, 8:16], cand[:, h, :])
                after(last)
                for h in range(HEADS):
                    last = nc.vector.max_index(best_at[:, h, 8:16], best[:, h, 8:16], cand[:, h, :])
                after(last)
                ring_free(dve, weight_ready, g)
                after(nc.vector.tensor_copy(zinv[:], best[:, :, 0]))
                nc.vector.tensor_tensor(best[:], best[:], zinv[:].unsqueeze(2).broadcast_to([P, HEADS, TOP]),
                                        ALU.subtract).then_inc(shifted, 1)
                for k in range(HEADS // 2):
                    two = slice(2 * k, 2 * k + 2)
                    shape = [P, 2, TOP, CANDS]
                    after(nc.vector.tensor_tensor(
                        hot[:], best_at[:, two, :].unsqueeze(3).broadcast_to(shape),
                        place[:].unsqueeze(1).unsqueeze(1).broadcast_to(shape), ALU.is_equal))
                    after(nc.vector.tensor_tensor(
                        hot[:], hot[:], cand_i[:, two, :].unsqueeze(2).broadcast_to(shape), ALU.mult))
                    after(nc.vector.tensor_reduce(row_f[:, two, :], hot[:], AX.X, ALU.add))
                nc.vector.tensor_tensor(row_i[:, t % 3, :], row_f[:].rearrange("p h j -> p (h j)"),
                                        head_base[:].rearrange("p h j -> p (h j)"), ALU.add
                                        ).then_inc(row_i_ready, 1)
                dve.wait_ge(expo_ready, g + 1)
                after(nc.vector.tensor_reduce(zsum[:], expo[:], AX.X, ALU.add))
                nc.vector.reciprocal(zinv[:], zsum[:]).then_inc(rank_step, 1)
                dve.wait_ge(rank_step, base + RANK_STEPS)
                nc.vector.tensor_tensor(weight[:, t % 3, :, :], expo[:],
                                        zinv[:].unsqueeze(2).broadcast_to([P, HEADS, TOP]), ALU.mult
                                        ).then_inc(weight_ready, 1)
                assert count[0] == RANK_STEPS - 1, count

            def heads(kind, b, t, hp):
                g = TILES * b + t
                for h in (2 * hp, 2 * hp + 1):
                    dve.wait_ge(weight_ready, g + 1)
                    dve.wait_ge(gathered[h], 16 * TOP * (g + 1))
                    nc.vector.tensor_tensor(rows[:, h, :, :], rows[:, h, :, :],
                                            weight[:, t % 3, h, :].unsqueeze(2).broadcast_to([P, TOP, ROW]),
                                            ALU.mult).then_inc(weighted, 1)
                for h in (2 * hp, 2 * hp + 1):
                    full(kind, b, ("score", t, h))
                    nc.vector.tensor_reduce(nmax[:, h:h + 1], wide_flat[:, 0:(t + 1) * P], AX.X, ALU.max,
                                            negate=True).then_inc(max_ready, 1)

            def finish(g):
                dve.wait_ge(o_filled, g + 1)
                dve.wait_ge(o_normed, g)
                nc.vector.reciprocal(rinv[:], rsum[:]).then_inc(o_inv, 1)
                dve.wait_ge(o_inv, g + 1)
                nc.vector.tensor_tensor(o_n[:], attn[:].rearrange("p (h d) -> p h d", d=DIM),
                                        rinv[:].unsqueeze(2).broadcast_to([P, HEADS, DIM]), ALU.mult
                                        ).then_inc(o_normed, 1)
                dve.wait_ge(fin_filled, g + 1)
                dve.wait_ge(stored, 16 * g)
                nc.vector.tensor_tensor(out_s[:], res[:], attn[:, 0:DIM], ALU.add).then_inc(out_ready, 1)

            def turn(kind, b):
                i = 0 if kind == "first" else b + 1
                for name, a, n in stages(kind):
                    if name == "front":
                        front(kind, b, i)
                    elif name == "units":
                        units(i, a, n)
                    elif name == "chunk":
                        chunk(kind, b, i, a)
                    elif name == "norm":
                        layer_norm(kind, b, 2 * i + 1, 2, xn_t[:])
                    elif name == "rank":
                        rank(kind, b, a, TILES * b + a)
                    elif name == "heads":
                        heads(kind, b, a, n)
                    elif name == "finish":
                        finish(TILES * b + a)

            turn("first", 0)
            with dve.Fori(0, BATCH - 1) as b:
                turn("turn", b)
            turn("last", BATCH - 1)

        @block.tensor
        def _(pe):
            pe.wait_ge(weights_in, 16 * len(loads))
            for o in range(DIM):
                for late in range(2):
                    dst = wide_flat[CHANNELS * late:CHANNELS * late + CHANNELS, 0:512]
                    mm = nc.tensor.matmul(dst.rearrange("p (k o) -> p k o", o=DIM)[:, :, o], w18[:, o, :],
                                          dft_s[:, STRIDE * late:STRIDE * late + STRIDE], start=True, stop=True)
            mm.then_inc(wide_filled.sem, 1)
            pe.wait_ge(wide_drained.sem, wide_drained.after("first", 0, "weff"))
            for q in range(2 * HEADS):
                mm = nc.tensor.matmul(wide_flat[0:DIM, q * KEYS:(q + 1) * KEYS], wqpk_s[:, q, :], keys_s[:, q, :],
                                      start=True, stop=True)
            mm.then_inc(wide_filled.sem, 1)
            pe.wait_ge(set_up, SETUP_STEPS)

            def free_wide(kind, b, key):
                pe.wait_ge(wide_drained.sem, wide_drained.before(kind, b, key))
                plain(pe)

            def free_small(kind, b, key):
                pe.wait_ge(small_drained.sem, small_drained.before(kind, b, key))
                plain(pe)

            def over_chunks(kind, b, key, parts, lhs, rhs):
                free_wide(kind, b, key)
                for c in range(CHUNKS):
                    mm = nc.tensor.matmul(wide[0:parts, c, 0:CH], lhs, rhs[:, c * CH:(c + 1) * CH],
                                          start=True, stop=True)
                mm.then_inc(wide_filled.sem, 1)

            def layer_norm(kind, b, n, which):
                over_chunks(kind, b, f"mean{which}", DIM, mean_w[:], h_t[:])
                pe.wait_ge(squared, n + 1)
                plain(pe)
                over_chunks(kind, b, f"var{which}", DIM, mean_w[:], sq)

            def front(kind, b, i):
                for half in range(2):
                    pe.wait_ge(x_in[half], (32 + 16 * half) * (i + 1))
                    free_wide(kind, b, f"tok{half}")
                    for k in range(STRIDE):
                        mm = nc.tensor.matmul(wide[0:DIM, 0, :], w_eff[:, k, :], x2[:, k:64:STRIDE, :],
                                              start=(k == 0), stop=(k == STRIDE - 1))
                    mm.then_inc(wide_filled.sem, 1)
                pe.wait_ge(text_in, 16 * (i + 1))
                layer_norm(kind, b, 2 * i, 1)
                pe.wait_ge(normed, 2 * i + 1)
                over_chunks(kind, b, "skip", DIM, win[:, 0, :], x_c)
                over_chunks(kind, b, "u", P, win[:, 1:3, :], x_c)
                pe.wait_ge(convolved, TAPS * i + TAPS)
                over_chunks(kind, b, "bc", P, wbc[:], u_t[0:DIM, :])
                over_chunks(kind, b, "lam", P, wlam[:], u_t[0:DIM, :])
                pe.wait_ge(wide_drained.sem, wide_drained.after(kind, b, "bc"))

            def spread_state(dst, first, c):
                for j in range(2):
                    pick = ident[:, first + j:first + j + 1].broadcast_to([P, DIM])
                    mm = nc.tensor.matmul(dst[j * DIM:(j + 1) * DIM, 0:CH], pick, bc_t[:, c * CH:(c + 1) * CH],
                                          start=True, stop=True)
                return mm

            def units(i, u0, n):
                for s in range(u0, u0 + n + 4):
                    if s < u0 + n:
                        c, p = divmod(s, PAIRS)
                        ring_free(pe, bu_ready, UNITS * i + s)
                        spread_state(bwide, 2 * p, c).then_inc(b_ready, 1)
                    if u0 <= s - 3 < u0 + n:
                        u = s - 3
                        c, p = divmod(u, PAIRS)
                        ring_free(pe, cy_ready, UNITS * i + u)
                        spread_state(cwide, STATE + 2 * p, c).then_inc(c_ready, 1)
                    if u0 <= s - 4:
                        u = s - 4
                        c, p = divmod(u, PAIRS)
                        pe.wait_ge(cy_ready, UNITS * i + u + 1)
                        if p == 0:
                            ring_free(pe, gated, CHUNKS * i + c)
                        nc.tensor.matmul(ysum[0:DIM, 0:CH], fold[:], cy_r[u % 2], start=(p == 0),
                                         stop=(p == PAIRS - 1)).then_inc(y_summed, 1)

            def chunk(kind, b, i, c):
                pe.wait_ge(gated, CHUNKS * i + c + 1)
                free_small(kind, b, ("out", c))
                nc.tensor.matmul(small[0:DIM, 0:CH], wout[:], gy[:], start=True, stop=True
                                 ).then_inc(small_filled.sem, 1)

            def norm(kind, b, i):
                pe.wait_ge(small_drained.sem, small_drained.after(kind, b, ("out", CHUNKS - 1)))
                layer_norm(kind, b, 2 * i + 1, 2)

            def query(kind, b, t):
                pe.wait_ge(normed, 2 * b + 2)
                free_small(kind, b, ("q", t))
                tile = slice(t * P, (t + 1) * P)
                for hp in range(HEADS // 2):
                    mm = nc.tensor.matmul(small[:, hp * P:(hp + 1) * P], wq[:, hp * P:(hp + 1) * P],
                                          xn_t[:, tile], start=True, stop=True)
                mm.then_inc(small_filled.sem, 1)
                pe.wait_ge(h1_copied, b + 1)
                free_small(kind, b, ("res", t))
                nc.tensor.transpose(small[:, 0:DIM], h1_t[:, tile], ident[0:DIM, 0:DIM]
                                    ).then_inc(small_filled.sem, 1)

            def rank(kind, b, t, i):
                pe.wait_ge(normed, 2 * i + 2)
                free_wide(kind, b, ("sim", t))
                for n in range(2):
                    mm = nc.tensor.matmul(wide[:, n, :], xn_t[:, (t % TILES) * P:(t % TILES + 1) * P],
                                          wcomb[:, n * 512:(n + 1) * 512], start=True, stop=True)
                mm.then_inc(wide_filled.sem, 1)

            def scores(kind, b, t, h):
                hp, half = h // 2, DIM * (h % 2)
                free_wide(kind, b, ("score", t, h))
                n = (t + 1) * P
                for lo in range(0, n, 512):
                    hi = min(lo + 512, n)
                    mm = nc.tensor.matmul(wide_flat[:, lo:hi], q_t[half:half + DIM, hp, :],
                                          k_t[half:half + DIM, hp, lo:hi], start=True, stop=(hi < n))
                nc.tensor.matmul(wide_flat[:, n - P:n], ident[:], causal[:], start=False, stop=True
                                 ).then_inc(wide_filled.sem, 1)

            def turned(kind, b, t, h):
                free_wide(kind, b, ("turned", t, h))
                for j in range(t + 1):
                    mm = nc.tensor.transpose(wide_flat[:, j * P:(j + 1) * P], prob[:, j * P:(j + 1) * P], ident[:])
                mm.then_inc(wide_filled.sem, 1)

            def attend(kind, b, t, h):
                pe.wait_ge(wide_drained.sem, wide_drained.after(kind, b, ("turned", t, h)))
                if h == 0:
                    pe.wait_ge(out_ready, TILES * b + t)
                for j in range(t + 1):
                    mm = nc.tensor.matmul(attn[:, h * DIM:(h + 1) * DIM], prob_t[:, j * P:(j + 1) * P],
                                          vals[:, j, h, :], start=(j == 0), stop=(j == t))
                if h == HEADS - 1:
                    mm.then_inc(o_filled, 1)

            def heads(kind, b, t, hp):
                g = TILES * b + t
                for h in (2 * hp, 2 * hp + 1):
                    pe.wait_ge(weighted, HEADS * g + h + 1)
                    free_small(kind, b, ("kv", t, h))
                    for j in range(TOP):
                        mm = nc.tensor.matmul(small[:, 0:ROW], ident[:], rows[:, h, j, :], start=(j == 0),
                                              stop=(j == TOP - 1))
                    mm.then_inc(rows_summed[h], 1)
                free_small(kind, b, ("keys", t, hp))
                nc.tensor.transpose(small[:, 0:P], k_nat[:].rearrange("p h d -> p (h d)"), ident[:]
                                    ).then_inc(small_filled.sem, 1)
                pe.wait_ge(small_drained.sem, small_drained.after(kind, b, ("keys", t, hp)))
                scores(kind, b, t, 2 * hp)
                turned(kind, b, t, 2 * hp)
                scores(kind, b, t, 2 * hp + 1)
                attend(kind, b, t, 2 * hp)
                turned(kind, b, t, 2 * hp + 1)
                attend(kind, b, t, 2 * hp + 1)

            def finish(g):
                pe.wait_ge(o_normed, g + 1)
                for c in range(HEADS // 2):
                    mm = nc.tensor.transpose(attn[:, c * P:(c + 1) * P],
                                             o_n[:].rearrange("p h d -> p (h d)")[:, c * P:(c + 1) * P], ident[:])
                mm.then_inc(o_turned, 1)
                pe.wait_ge(o_t_ready, g + 1)
                for c in range(HEADS // 2):
                    mm = nc.tensor.matmul(attn[:, 0:DIM], o_t[:, c, :], wo[:, c, :], start=(c == 0),
                                          stop=(c == HEADS // 2 - 1))
                mm.then_inc(fin_filled, 1)

            def turn(kind, b):
                i = 0 if kind == "first" else b + 1
                for name, a, n in stages(kind):
                    if name == "front":
                        front(kind, b, i)
                    elif name == "units":
                        units(i, a, n)
                    elif name == "chunk":
                        chunk(kind, b, i, a)
                    elif name == "norm":
                        norm(kind, b, i)
                    elif name == "query":
                        query(kind, b, a)
                    elif name == "rank":
                        rank(kind, b, a, b + a // TILES)
                    elif name == "heads":
                        heads(kind, b, a, n)
                    elif name == "finish":
                        finish(TILES * b + a)

            turn("first", 0)
            with pe.Fori(0, BATCH - 1) as b:
                turn("turn", b)
            turn("last", BATCH - 1)


EXP_AND_LN = "natural_log_exp_and_others"
SERIES = (17, 15, 13, 11, 9, 7, 5, 3)
SETUP_STEPS = 12 + len(SERIES)


def dft_table():
    angle = 2 * np.pi * np.arange(FREQS)[:, None] * np.arange(PATCH)[None, :] / PATCH
    return (np.concatenate([np.cos(angle), -np.sin(angle)]) / np.sqrt(PATCH)).astype(np.float32)


def kernel(**inputs):
    import concourse.bacc as bacc
    from concourse.bass_utils import run_bass_kernel_spmd

    a = {k: np.asarray(v) for k, v in inputs.items()}
    col = lambda v: v.reshape(-1, 1)
    arrays = {
        "x": a["x"],
        "text": a["txt"],
        "text_t": a["txt"].transpose(0, 2, 1),
        "w_tok": a["L0_tok_W"].reshape(DIM, 2 * FREQS, CHANNELS).transpose(1, 0, 2),
        "dft": dft_table(),
        "w_in": a["L0_attn_W_in"].T,
        "conv_w": a["L0_attn_conv_w"].reshape(DIM, TAPS),
        "conv_b": col(a["L0_attn_conv_b"]),
        "w_bc": a["L0_attn_W_bc"].T,
        "b_bc": col(a["L0_attn_b_bc"]),
        "w_lam": a["L0_attn_W_lam"].T,
        "b_lam": col(a["L0_attn_b_lam"]),
        "decay": a["L0_attn_A"].reshape(PAIRS, 2, DIM).transpose(1, 2, 0).reshape(P, PAIRS),
        "w_out": a["L0_attn_W_out"].T,
        "w_qpk": a["L0_ffn_Wq_pk"].reshape(DIM, 2 * HEADS, KEYDIM).transpose(2, 1, 0),
        "keys": a["L0_ffn_pk_keys"].transpose(3, 0, 2, 1).reshape(KEYDIM, 2 * HEADS, KEYS),
        "w_q": a["L0_ffn_Wq"],
        "tables": np.concatenate([a["L0_ffn_keys_table"], a["L0_ffn_values_table"]], axis=1),
        "w_o": a["L0_ffn_Wo"].reshape(HEADS * DIM // P, P, DIM).transpose(1, 0, 2),
        "ident_d": np.eye(P, dtype=np.float32),
        "fold_d": np.tile(np.eye(DIM, dtype=np.float32), (2, 1)),
        "causal_d": np.triu(np.full((P, P), MASKED, np.float32), 1),
    }
    nc = bacc.Bacc("TRN2", target_bir_lowering=False, num_devices=1)
    arrays = {f"in_{k}": np.ascontiguousarray(v) for k, v in arrays.items()}
    args = {k[3:]: nc.dram_tensor(k, v.shape, mybir.dt.from_np(v.dtype), kind="ExternalInput").ap()
            for k, v in arrays.items()}
    args["out"] = nc.dram_tensor("out", (BATCH, LEN, DIM), F32, kind="ExternalOutput").ap()
    program(nc, **args)
    r = run_bass_kernel_spmd(nc, [arrays], core_ids=[0])
    return r.results[0]["out"]
```

```python
from contextlib import ExitStack

import numpy as np

import concourse.bass as bass
from concourse import mybir

F32 = mybir.dt.float32
U32 = mybir.dt.uint32
ALU = mybir.AluOpType
ACT = mybir.ActivationFunctionType
AX = mybir.AxisListType

P = 128
BATCH, CHANNELS, TIME, VARS = 4, 64, 128, 64
PATCH, STRIDE = 16, 8
PATCHES = TIME // STRIDE
FREQS = PATCH // 2 + 1
DIM = 64
TEXT = 128
TOKENS = VARS * PATCHES
LEN = TOKENS + TEXT
TILES = LEN // P
STATE = 64
TAPS = 4
PAIRS = STATE // 2
CHUNKS = 3
CH = LEN // CHUNKS
UNITS = CHUNKS * PAIRS
LAG = 4
HEADS = 8
KEYS = 64
TOP = 16
FOLDED = TOP // 2
KEYDIM = 32
ROW = 2 * DIM
LIMITS = [TOP // (a + 1) for a in range(TOP)]
PLACES = [sum(LIMITS[:a]) for a in range(TOP)]
CANDS = sum(LIMITS)
LOWEST = float(np.finfo(np.float32).min)
MASKED = -1e30
LN_EPS = 1e-5
DECAY_EPS = 1e-6
PICKS = 4
CREDIT = 2
RANK_STEPS = 25


def ticks_in(t, s):
    return ((4, 3, 3, 3, 3), (4, 3, 3, 3, 3), (3, 3, 3, 3, 2), (3, 3, 3, 3, 2), (4, 0, 0, 0, 0),
            (3, 3, 2, 2, 2), (3, 3, 2, 2, 2), (3, 3, 2, 2, 2), (0, 0, 0, 0, 0))[t][s]


def stages(kind):
    if kind == "first":
        for part in range(3):
            yield "front", part, 0
        yield "ticks", 0, range(PAIRS + LAG)
        yield "norm", 0, 0
        yield "sim", 0, 0
        for s in range(4):
            yield "rank", 0, s
        yield "sim", 1, 0
        return
    ahead = kind == "turn"
    tick = PAIRS + LAG
    for t in range(TILES):
        yield "query", t, 0
        for s in range(HEADS // 2 + 1):
            n = ticks_in(t, s) if ahead or tick < UNITS + LAG else 0
            yield "step", t, (s, range(tick, tick + n))
            tick += n
            if s == 0 and t:
                yield "close", t - 1, 0
            if t == 4 and 1 <= s <= 3 and ahead:
                yield "front", s - 1, 0
            if n and tick % (UNITS + LAG) in (PAIRS + LAG, 2 * PAIRS + LAG, 0):
                yield "norm", ((tick - LAG) // PAIRS - 1) % CHUNKS, 0
        if ahead or t + 2 < TILES:
            yield "sim", t + 2, 0
        yield "finish", t, 0
    yield "close", TILES - 1, 0


def wide_steps(kind):
    out = ["weff", "wcomb"] if kind == "first" else []
    for name, a, s in stages(kind):
        if name == "front":
            out += (["tok0"], ["tok1", "mean", "var"], ["skip", "u", "bc", "lam"])[a]
        elif name == "norm":
            out += [f"mean{a}", f"var{a}"]
        elif name == "sim":
            out += [("sim", a)]
        elif name == "step" and s[0]:
            s = s[0]
            out += [(what, a, h) for h in (2 * s - 2, 2 * s - 1) for what in ("score", "turned")]
    return out


def small_steps(kind, filled):
    out = []
    for name, a, s in stages(kind):
        if name == "query":
            out += [("q", a), ("res", a)]
        elif name == "norm":
            out += [("out", a)]
        elif name == "step" and s[0] < HEADS // 2:
            s = s[0]
            out += [] if filled else [("kv", a, 2 * s), ("kv", a, 2 * s + 1)]
            out += [("keys", a, s)]
    return out


class Count:

    def __init__(self, sem, lists):
        self.sem = sem
        self.at = {kind: {key: i for i, key in enumerate(steps)} for kind, steps in lists.items()}
        self.first, self.turn = len(lists["first"]), len(lists["turn"])

    def before(self, kind, b, key):
        i = self.at[kind][key]
        return i if kind == "first" else b * self.turn + (self.first + i)

    def after(self, kind, b, key):
        i = self.at[kind][key] + 1 if key else 0
        return i if kind == "first" else b * self.turn + (self.first + i)


def program(nc, x, text, text_t, w_tok, dft, w_in, conv_w, conv_b, w_bc, b_bc, w_lam, b_lam, decay, w_out,
            w_qpk, keys, w_q, tables, w_o, ident_d, fold_d, causal_d, out):
    kinds = ("first", "turn", "last")
    with ExitStack() as ctx:
        def sb(name, shape, dt=F32):
            return ctx.enter_context(nc.sbuf_tensor(name, shape, dt))

        def ps(name, shape):
            return ctx.enter_context(nc.psum_tensor(name, shape, F32))

        def sem(name):
            return ctx.enter_context(nc.semaphore(name))

        wide = ps("wide", [P, 3, 512])
        small = ps("small", [P, 512])
        attn = ps("attn", [P, 512])
        bwide = ps("bwide", [P, 512])
        cwide = ps("cwide", [P, 512])
        ysum = ps("ysum", [P, 512])
        wide_flat = wide[:].rearrange("p a b -> p (a b)")

        ident = sb("ident", [P, P])
        fold = sb("fold", [P, DIM])
        causal = sb("causal", [P, P])
        dft_s = sb("dft_s", [2 * FREQS, PATCH])
        mean_w = sb("mean_w", [DIM, DIM])
        one_eps = sb("one_eps", [P, 1])
        ln_eps = sb("ln_eps", [P, 1])
        w_eff = sb("w_eff", [P, STRIDE, DIM])
        win = sb("win", [DIM, 3, DIM])
        cw = sb("cw", [P, TAPS])
        cb = sb("cb", [P, 1])
        wbc = sb("wbc", [DIM, P])
        bbc = sb("bbc", [P, 1])
        wlam = sb("wlam", [DIM, 2, DIM])
        blam = sb("blam", [P, 1])
        nblam = sb("nblam", [P, 1])
        wout = sb("wout", [P, DIM])[DIM:P, :]
        coef = sb("coef", [P, PAIRS])
        coef2 = sb("coef2", [P, PAIRS])
        wcomb = sb("wcomb", [DIM, 2 * HEADS * KEYS])
        wq = sb("wq", [DIM, HEADS * DIM])
        wo = sb("wo", [P, HEADS * DIM // P, DIM])
        head_base = sb("head_base", [P, HEADS], U32)
        place = sb("place", [P, CANDS], U32)

        h_both = sb("h_both", [P, LEN])
        h_t, h1_t = h_both[0:DIM, :], h_both[DIM:P, :]
        upad = sb("upad", [P, LEN + TAPS - 1])
        x_c = upad[0:DIM, TAPS - 1:]
        bc_t = sb("bc_t", [P, LEN])
        u_t = sb("u_t", [P, LEN])
        sig = sb("sig", [P, LEN])
        xn_gate = sb("xn_gate", [P, LEN])
        xn_t, gate = xn_gate[0:DIM, :], xn_gate[DIM:P, :]
        carry = sb("carry", [P, PAIRS])
        gy = sb("gy", [P, CH])[DIM:P, :]
        arena = sb("arena", [P, 12 * CH])
        x2 = arena[:, 0:64 * VARS].rearrange("p (t v) -> p t v", v=VARS)

        def ring(first, n):
            return [arena[:, (first + i) * CH:(first + i + 1) * CH] for i in range(n)]

        lam_r, v_r, z_r, hs_r, cy_r = ring(0, 3), ring(3, 3), ring(6, 2), ring(8, 2), ring(10, 2)
        norm_all = (x_c, bc_t[0:DIM, :], bc_t[0:DIM, :], u_t[0:DIM, :])
        xc_c, sq_c, rr_c = (sb(name, [DIM, CH])[:] for name in ("xc_c", "sq_c", "rr_c"))
        norm_chunk = (xc_c, sq_c, sq_c, rr_c)
        pick = [sb(f"pick{i}", [P, 2, DIM]) for i in range(PICKS)]

        sims = sb("sims", [P, 2 * HEADS, KEYS])
        top_v = sb("top_v", [P, 2 * HEADS, TOP])
        top_i = sb("top_i", [P, 2 * HEADS, TOP], U32)
        idx1 = sb("idx1", [P, HEADS, TOP])
        cand = sb("cand", [P, HEADS, CANDS])
        cand_i = sb("cand_i", [P, HEADS, CANDS])
        best = sb("best", [P, HEADS, TOP])
        best_at = sb("best_at", [P, HEADS, TOP], U32)
        hot = sb("hot", [P, 2, TOP, CANDS])
        row_f = sb("row_f", [P, HEADS, TOP])
        expo = sb("expo", [P, HEADS, TOP])
        zsum = sb("zsum", [P, HEADS])
        zinv = sb("zinv", [P, HEADS])
        row_i = sb("row_i", [P, 3, HEADS * TOP], U32)
        weight = sb("weight", [P, 3, HEADS, TOP])

        rows = sb("rows", [P, HEADS, TOP, ROW])
        vals = sb("vals", [P, TILES, HEADS, DIM])
        k_nat = sb("k_nat", [P, 2, DIM])
        k_t = sb("k_t", [P, HEADS // 2, LEN])
        q_t = sb("q_t", [P, HEADS // 2, P])
        res = sb("res", [P, 3, DIM])
        nmax = sb("nmax", [P, HEADS])
        rsum = sb("rsum", [P, HEADS])
        rinv = sb("rinv", [P, HEADS])
        prob = sb("prob", [P, LEN])
        prob_t = sb("prob_t", [P, LEN])
        o_n = sb("o_n", [P, HEADS, DIM])
        o_t = sb("o_t", [P, HEADS * DIM // P, P])
        out_s = sb("out_s", [P, DIM])

        rows_flat = rows[:].rearrange("p h j r -> p (h j r)")
        w18 = rows_flat[0:2 * FREQS, 0:DIM * CHANNELS].rearrange("r (o c) -> r o c", o=DIM)
        wqpk_s = rows_flat[0:KEYDIM, 4096:5120].rearrange("d (g i) -> d g i", i=DIM)
        keys_s = rows_flat[0:KEYDIM, 5120:6144].rearrange("d (g k) -> d g k", k=KEYS)

        raw_a, *sp = [rows_flat[:, 6144 + i * PAIRS:6144 + (i + 1) * PAIRS] for i in range(5)]

        weights_in = sem("weights_in")
        passed = sem("passed")
        set_up = sem("set_up")
        spread = sem("spread")
        pos_ready = sem("pos_ready")
        x_in = [sem("x_in0"), sem("x_in1")]
        text_in = sem("text_in")
        wide_filled = Count(sem("wide_filled"), {k: wide_steps(k) for k in kinds})
        wide_drained = Count(sem("wide_drained"), {k: wide_steps(k) for k in kinds})
        small_filled = Count(sem("small_filled"), {k: small_steps(k, True) for k in kinds})
        small_drained = Count(sem("small_drained"), {k: small_steps(k, False) for k in kinds})
        centred = sem("centred")
        squared = sem("squared")
        log_ready = sem("log_ready")
        inv_ready = sem("inv_ready")
        newton = sem("newton")
        normed = sem("normed")
        convolved = sem("convolved")
        sig_step = sem("sig_step")
        lam_ready = sem("lam_ready")
        lam2_ready = sem("lam2_ready")
        z_log = sem("z_log")
        picked = sem("picked")
        z_ready = sem("z_ready")
        b_ready = sem("b_ready")
        c_ready = sem("c_ready")
        bu_ready = sem("bu_ready")
        scaled = sem("scaled")
        scanned = sem("scanned")
        carried = sem("carried")
        cy_ready = sem("cy_ready")
        y_summed = sem("y_summed")
        gated = sem("gated")
        h1_copied = sem("h1_copied")
        rank_step = sem("rank_step")
        shifted = sem("shifted")
        expo_ready = sem("expo_ready")
        row_i_ready = sem("row_i_ready")
        weight_ready = sem("weight_ready")
        gathered = [sem(f"gathered{h}") for h in range(HEADS)]
        weighted = sem("weighted")
        halved = sem("halved")
        rows_summed = [sem(f"rows_summed{h}") for h in range(HEADS)]
        max_ready = sem("max_ready")
        o_filled = sem("o_filled")
        o_inv = sem("o_inv")
        o_normed = sem("o_normed")
        o_turned = sem("o_turned")
        o_t_ready = sem("o_t_ready")
        fin_filled = sem("fin_filled")
        out_ready = sem("out_ready")
        stored = sem("stored")

        loads = [
            (ident[:], ident_d), (fold[:], fold_d), (causal[:], causal_d), (dft_s[:], dft),
            (w18, w_tok), (wqpk_s, w_qpk), (keys_s, keys),
            (win[:, 0, :], w_in[:, 0:DIM]), (win[:, 1, :], w_in[:, DIM:]), (win[:, 2, :], w_in[:, DIM:]),
            (cw[0:DIM, :], conv_w), (cw[DIM:P, :], conv_w), (cb[0:DIM, :], conv_b), (cb[DIM:P, :], conv_b),
            (wbc[:], w_bc), (bbc[:], b_bc), (wlam[:, 0, :], w_lam), (wlam[:, 1, :], w_lam),
            (blam[0:DIM, :], b_lam), (blam[DIM:P, :], b_lam), (wout, w_out), (raw_a, decay),
            (wq[:], w_q), (wo[:], w_o),
        ]

        def ring_free(eng, s, value):
            if not isinstance(value, int) or value > 0:
                eng.wait_ge(s, value)

        def plain(eng):
            eng.sem_inc(passed, 1)

        def wide_view(parts):
            return wide[0:parts, :, 0:CH]

        def in_chunks(ap):
            return ap.rearrange("p (c k) -> p c k", k=CH)

        def norm_of(i, c):
            return (1 + CHUNKS) * i + (0 if c is None else 1 + c)

        def norm_parts(c):
            if c is None:
                return ("mean", "var"), norm_all, slice(0, LEN), wide[0:DIM, :, 0:CH]
            return (f"mean{c}", f"var{c}"), norm_chunk, slice(c * CH, (c + 1) * CH), wide[0:DIM, 0:1, 0:CH]

        def tick_batch(b, v):
            return (b, v) if v < UNITS + LAG else (b + 1, v - UNITS - LAG)

        block = ctx.enter_context(nc.Block())

        @block.sync
        def _(sync):
            for dst, src in loads:
                sync.dma_start(dst, src).then_inc(weights_in, 16)

            def load_half(kind, b, i, half):
                lo = 64 * half
                if half:
                    sync.wait_ge(wide_filled.sem, wide_filled.after(kind, b, "tok0"))
                else:
                    ring_free(sync, normed, norm_of(i, None))
                sync.dma_start(x2[0:CHANNELS, :, :], x[i, :, lo:lo + 64, :]).then_inc(x_in[half], 16)
                if half == 0:
                    sync.dma_start(x2[CHANNELS:P, :, :],
                                   x[i, :, STRIDE:STRIDE + 64, :]).then_inc(x_in[0], 16)
                    ring_free(sync, h1_copied, CHUNKS * i)
                    sync.dma_start(h_t[:, TOKENS:LEN], text_t[i]).then_inc(text_in, 16)
                else:
                    last = 64 - STRIDE
                    sync.dma_start(x2[CHANNELS:P, 0:last, :],
                                   x[i, :, lo + STRIDE:TIME, :]).then_inc(x_in[1], 16)
                    sync.dma_start(x2[CHANNELS:P, last:64, :],
                                   x[i, :, TIME - 1:TIME, :].broadcast_to([CHANNELS, STRIDE, VARS])
                                   ).then_inc(x_in[1], 16)

            def store(b, t):
                sync.wait_ge(out_ready, TILES * b + t + 1 + CREDIT)
                sync.dma_start(out[b, t * P:(t + 1) * P, :], out_s[:]).then_inc(stored, 16)

            sync.sem_inc(stored, 16 * CREDIT)
            for half in range(2):
                load_half("first", 0, 0, half)
            with sync.Fori(0, BATCH - 1) as b:
                for t in range(TILES):
                    for half in range(2) if t == 4 else ():
                        load_half("turn", b, b + 1, half)
                    store(b, t)
            for t in range(TILES):
                store(BATCH - 1, t)
            sync.wait_ge(stored, 16 * (TILES * BATCH + CREDIT))

        @block.gpsimd
        def _(pool):
            nc.gpsimd.iota(head_base[:], [[KEYS * KEYS, HEADS]], base=0,
                           channel_multiplier=0).then_inc(pos_ready, 1)
            nc.gpsimd.iota(place[:], [[1, CANDS]], base=0, channel_multiplier=0).then_inc(pos_ready, 1)
            pool.wait_ge(wide_filled.sem, wide_filled.after("first", 0, "wcomb"))
            pool.wait_ge(set_up, SETUP_STEPS)

            def gather(b):
                for t in range(TILES):
                    g = TILES * b + t
                    pool.wait_ge(row_i_ready, g + 1)
                    for h in range(HEADS):
                        pool.wait_ge(rows_summed[h], g + CREDIT)
                        plain(pool)
                        for j in range(TOP):
                            at = h * TOP + j
                            nc.gpsimd.indirect_dma_start(
                                rows[:, h, j, :], None, tables,
                                bass.IndirectOffsetOnAxis(ap=row_i[:, t % 3, at:at + 1], axis=0),
                            ).then_inc(gathered[h], 16)

            with pool.Fori(0, BATCH - 1) as b:
                gather(b)
            gather(BATCH - 1)

        @block.scalar
        def _(act):
            nc.scalar.preload_act_table_set(EXP_AND_LN)
            act.wait_ge(weights_in, 16 * len(loads))
            act.wait_ge(wide_filled.sem, wide_filled.after("first", 0, "weff"))
            nc.scalar.copy(w_eff[:].rearrange("p k o -> p (k o)"), wide_flat[:, 0:512]).then_inc(wide_drained.sem, 1)
            act.wait_ge(wide_filled.sem, wide_filled.after("first", 0, "wcomb"))
            nc.scalar.copy(wcomb[:], wide_flat[0:DIM, 0:1024]).then_inc(wide_drained.sem, 1)
            act.wait_ge(set_up, 2)
            nc.scalar.activation(sp[1], sp[0], ACT.Exp).then_inc(spread, 1)
            act.wait_ge(set_up, SETUP_STEPS)

            def full(kind, b, key):
                act.wait_ge(wide_filled.sem, wide_filled.after(kind, b, key))

            def inverse_root(kind, b, i, c):
                (_, var), (_, _, inv, _), _, view = norm_parts(c)
                n = norm_of(i, c)
                full(kind, b, var)
                nc.scalar.activation(in_chunks(inv), view, ACT.Ln, bias=ln_eps[0:DIM, :]
                                     ).then_inc(log_ready, 1)
                act.wait_ge(log_ready, n + 1)
                nc.scalar.activation(inv, inv, ACT.Exp, scale=-0.5).then_inc(inv_ready, 1)

            def front(kind, b, i, part):
                if part < 2:
                    full(kind, b, f"tok{part}")
                    if part == 0:
                        ring_free(act, h1_copied, CHUNKS * i)
                    dst = h_t[:, 0:TOKENS].rearrange("o (v n) -> o n v", n=PATCHES)[:, 8 * part:8 * part + 8, :]
                    src = wide[0:DIM, 0, :].rearrange("o (n v) -> o n v", v=VARS)
                    nc.scalar.copy(dst, src).then_inc(wide_drained.sem, 1)
                    if part:
                        inverse_root(kind, b, i, None)
                    return
                full(kind, b, "skip")
                nc.scalar.activation(in_chunks(gate), wide[DIM:P, :, 0:CH], ACT.Gelu).then_inc(wide_drained.sem, 1)
                nc.scalar.preload_act_table_set(EXP_AND_LN)
                full(kind, b, "u")
                nc.scalar.copy(in_chunks(upad[:, TAPS - 1:]), wide_view(P)).then_inc(wide_drained.sem, 1)
                full(kind, b, "bc")
                nc.scalar.activation(in_chunks(bc_t[:]), wide_view(P), ACT.Identity, bias=bbc[:]
                                     ).then_inc(wide_drained.sem, 1)
                full(kind, b, "lam")
                nc.scalar.activation(in_chunks(sig[:]), wide_view(P), ACT.Exp, bias=nblam[:], scale=-1.0
                                     ).then_inc(wide_drained.sem, 1)

            def tick(i, u):
                if u >= UNITS:
                    return
                c, p = divmod(u, PAIRS)
                done = UNITS * i + u
                s = sig[:, c * CH:(c + 1) * CH]
                if u == 0:
                    act.wait_ge(sig_step, 2 * i + 2)
                ring_free(act, c_ready, done - PICKS + 1)
                nc.scalar.copy(pick[u % PICKS][:], fold[:, 2 * p:2 * p + 2].unsqueeze(2).broadcast_to([P, 2, DIM])
                               ).then_inc(picked, 1)
                ring_free(act, scanned, done - 2)
                nc.scalar.activation(lam_r[u % 3], s, ACT.Exp, scale=coef[:, p:p + 1]).then_inc(lam_ready, 1)
                ring_free(act, scaled, done - 1)
                nc.scalar.activation(z_r[u % 2], s, ACT.Exp, scale=coef2[:, p:p + 1]).then_inc(lam2_ready, 1)
                act.wait_ge(lam2_ready, done + 1)
                nc.scalar.activation(z_r[u % 2], z_r[u % 2], ACT.Ln, bias=one_eps[:], scale=-1.0
                                     ).then_inc(z_log, 1)
                act.wait_ge(z_log, done + 1)
                nc.scalar.activation(z_r[u % 2], z_r[u % 2], ACT.Exp, scale=0.5).then_inc(z_ready, 1)

            def norm(kind, b, i, c):
                inverse_root(kind, b, i, c)
                act.wait_ge(normed, norm_of(i, c) + 1)
                cols = norm_parts(c)[2]
                nc.scalar.copy(h1_t[:, cols], h_t[:, cols]).then_inc(h1_copied, 1)

            def query(kind, b, t):
                act.wait_ge(small_filled.sem, small_filled.after(kind, b, ("q", t)))
                nc.scalar.mul(q_t[:].rearrange("p a t -> p (a t)"), small[:], DIM ** -0.5
                              ).then_inc(small_drained.sem, 1)
                act.wait_ge(small_filled.sem, small_filled.after(kind, b, ("res", t)))
                act.wait_ge(out_ready, TILES * b + t - 1 + CREDIT)
                nc.scalar.copy(res[:, t % 3, :], small[:, 0:DIM]).then_inc(small_drained.sem, 1)

            def sim(kind, b, t, g):
                full(kind, b, ("sim", t))
                ring_free(act, rank_step, RANK_STEPS * g)
                nc.scalar.copy(sims[:].rearrange("p g k -> p (g k)"), wide_flat[:, 0:1024]
                               ).then_inc(wide_drained.sem, 1)

            def exponentials(g):
                act.wait_ge(shifted, g + 1)
                ring_free(act, weight_ready, g)
                nc.scalar.activation(expo[:], best[:], ACT.Exp).then_inc(expo_ready, 1)

            def exponential_row(g, t, h):
                act.wait_ge(max_ready, HEADS * g + h + 1)
                nc.scalar.activation(prob[:, 0:(t + 1) * P], wide_flat[:, 0:(t + 1) * P], ACT.Exp,
                                     bias=nmax[:, h:h + 1], accum_out=rsum[:, h:h + 1]
                                     ).then_inc(wide_drained.sem, 1)

            def turned_copy(kind, b, t, h):
                full(kind, b, ("turned", t, h))
                n = (t + 1) * P
                nc.scalar.copy(prob_t[:, 0:n], wide_flat[:, 0:n]).then_inc(wide_drained.sem, 1)

            def row_copy(g, t, h):
                act.wait_ge(rows_summed[h], g + 1 + CREDIT)
                nc.scalar.copy(vals[:, t, h, :], small[:, DIM:ROW])
                nc.scalar.copy(k_nat[:, h % 2, :], small[:, 0:DIM]).then_inc(small_drained.sem, 1)

            def step(kind, b, t, s, ticks):
                g = TILES * b + t
                old, new = (2 * s - 2, 2 * s - 1), (2 * s, 2 * s + 1)
                attending, summing = s > 0, s < HEADS // 2

                def scan(k):
                    if k < len(ticks):
                        tick(*tick_batch(b, ticks[k]))

                if attending:
                    exponential_row(g, t, old[0])
                scan(0)
                if attending:
                    turned_copy(kind, b, t, old[0])
                if summing:
                    row_copy(g, t, new[0])
                scan(1)
                if attending:
                    exponential_row(g, t, old[1])
                if summing:
                    row_copy(g, t, new[1])
                    act.wait_ge(small_filled.sem, small_filled.after(kind, b, ("keys", t, s)))
                    nc.scalar.copy(k_t[:, s, t * P:(t + 1) * P], small[:, 0:P]).then_inc(small_drained.sem, 1)
                scan(2)
                if attending:
                    turned_copy(kind, b, t, old[1])
                scan(3)
                if s == 2 and (kind == "turn" or t + 1 < TILES):
                    exponentials(g + 1)

            def finish(g):
                act.wait_ge(o_turned, g + 1)
                nc.scalar.copy(o_t[:].rearrange("p c t -> p (c t)"), attn[:]).then_inc(o_t_ready, 1)

            def turn(kind, b):
                for name, a, n in stages(kind):
                    i = b if kind == "first" or name == "norm" and a else b + 1
                    if name == "front":
                        front(kind, b, i, a)
                    elif name == "ticks":
                        for v in n:
                            tick(0, v)
                    elif name == "norm":
                        norm(kind, b, i, a)
                    elif name == "query":
                        query(kind, b, a)
                    elif name == "sim":
                        sim(kind, b, a, TILES * b + a)
                    elif name == "rank" and n == 3:
                        exponentials(0)
                    elif name == "step":
                        step(kind, b, a, *n)
                    elif name == "finish":
                        finish(TILES * b + a)

            turn("first", 0)
            with act.Fori(0, BATCH - 1) as b:
                turn("turn", b)
            turn("last", BATCH - 1)

        @block.vector
        def _(dve):
            nc.vector.memset(mean_w[:], 1.0 / DIM)
            nc.vector.memset(upad[:, 0:TAPS - 1], 0.0)
            nc.vector.memset(one_eps[:], 1.0 + DECAY_EPS)
            nc.vector.memset(ln_eps[:], LN_EPS)
            dve.wait_ge(weights_in, 16 * len(loads))
            count = [0]

            def step(ins):
                count[0] += 1
                ins.then_inc(set_up, 1)
                dve.wait_ge(set_up, count[0])

            step(nc.vector.tensor_scalar(sp[0], raw_a, -1.0, None, ALU.mult))
            step(nc.vector.tensor_tensor(sp[0], sp[0], raw_a, ALU.min))
            dve.wait_ge(spread, 1)
            step(nc.vector.tensor_scalar(sp[2], sp[1], 2.0, None, ALU.add))
            step(nc.vector.reciprocal(sp[2], sp[2]))
            step(nc.vector.tensor_tensor(sp[1], sp[1], sp[2], ALU.mult))
            step(nc.vector.tensor_tensor(sp[2], sp[1], sp[1], ALU.mult))
            step(nc.vector.tensor_scalar(sp[3], sp[2], 1.0 / SERIES[0], None, ALU.mult))
            for k in SERIES[1:]:
                step(nc.vector.scalar_tensor_tensor(sp[3], sp[3], 1.0 / k, sp[2], ALU.add, ALU.mult))
            step(nc.vector.scalar_tensor_tensor(sp[3], sp[3], 1.0, sp[1], ALU.add, ALU.mult))
            step(nc.vector.tensor_scalar(sp[0], raw_a, 0.0, None, ALU.max))
            step(nc.vector.scalar_tensor_tensor(sp[3], sp[3], 2.0, sp[0], ALU.mult, ALU.add))
            step(nc.vector.tensor_scalar(coef[:], sp[3], -8.0, None, ALU.mult))
            step(nc.vector.tensor_scalar(coef2[:], sp[3], -16.0, None, ALU.mult))
            step(nc.vector.tensor_scalar(nblam[:], blam[:], -1.0, None, ALU.mult))
            assert count[0] == SETUP_STEPS
            dve.wait_ge(pos_ready, 2)

            def full(kind, b, key):
                dve.wait_ge(wide_filled.sem, wide_filled.after(kind, b, key))

            def layer_norm(kind, b, i, c, dst):
                (mean, var), (xc, sq, inv, rr), cols, view = norm_parts(c)
                n = norm_of(i, c)
                full(kind, b, mean)
                ring_free(dve, normed, n)
                nc.vector.tensor_tensor(in_chunks(xc), in_chunks(h_t[:, cols]), view, ALU.subtract
                                        ).then_inc(wide_drained.sem, 1)
                dve.wait_ge(wide_drained.sem, wide_drained.after(kind, b, mean))
                nc.vector.tensor_tensor(sq, xc, xc, ALU.mult).then_inc(squared, 1)
                full(kind, b, var)
                dve.wait_ge(inv_ready, n + 1)
                nc.vector.tensor_tensor(rr, inv, inv, ALU.mult).then_inc(newton, 1)
                dve.wait_ge(newton, 3 * n + 1)
                nc.vector.scalar_tensor_tensor(in_chunks(rr), view, LN_EPS, in_chunks(rr),
                                               ALU.add, ALU.mult).then_inc(wide_drained.sem, 1)
                dve.wait_ge(wide_drained.sem, wide_drained.after(kind, b, var))
                nc.vector.tensor_scalar(rr, rr, -0.5, 1.5, ALU.mult, ALU.add).then_inc(newton, 1)
                dve.wait_ge(newton, 3 * n + 2)
                nc.vector.tensor_tensor(rr, rr, inv, ALU.mult).then_inc(newton, 1)
                dve.wait_ge(newton, 3 * n + 3)
                nc.vector.tensor_tensor(dst, xc, rr, ALU.mult).then_inc(normed, 1)

            def front(kind, b, i, part):
                if part == 1:
                    dve.wait_ge(text_in, 16 * (i + 1))
                    layer_norm(kind, b, i, None, x_c)
                if part < 2:
                    return
                dve.wait_ge(wide_drained.sem, wide_drained.after(kind, b, "u"))
                nc.vector.tensor_scalar(u_t[:], upad[:, 0:LEN], cw[:, 0:1], cb[:, 0:1], ALU.mult, ALU.add
                                        ).then_inc(convolved, 1)
                for k in range(1, TAPS):
                    dve.wait_ge(convolved, TAPS * i + k)
                    nc.vector.scalar_tensor_tensor(u_t[:], upad[:, k:k + LEN], cw[:, k:k + 1], u_t[:],
                                                   ALU.mult, ALU.add).then_inc(convolved, 1)
                dve.wait_ge(wide_drained.sem, wide_drained.after(kind, b, "lam"))
                nc.vector.tensor_scalar(sig[:], sig[:], 1.0, None, ALU.add).then_inc(sig_step, 1)
                dve.wait_ge(sig_step, 2 * i + 1)
                nc.vector.reciprocal(sig[:], sig[:]).then_inc(sig_step, 1)
                dve.wait_ge(convolved, TAPS * i + TAPS)
                plain(dve)

            def tick(i, v):
                u = v - 1
                if 0 <= u < UNITS:
                    c = u // PAIRS
                    done = UNITS * i + u
                    dve.wait_ge(b_ready, done + 1)
                    ring_free(dve, scanned, done - 2)
                    nc.vector.tensor_tensor(v_r[u % 3], bwide[:, 0:CH], u_t[:, c * CH:(c + 1) * CH],
                                            ALU.mult).then_inc(bu_ready, 1)
                u = v - 4
                if 0 <= u < UNITS:
                    p = u % PAIRS
                    done = UNITS * i + u
                    dve.wait_ge(scanned, done + 1)
                    nc.vector.tensor_copy(carry[:, p:p + 1], hs_r[u % 2][:, CH - 1:CH]).then_inc(carried, 1)
                    dve.wait_ge(c_ready, done + 1)
                    ring_free(dve, y_summed, done - 1)
                    nc.vector.tensor_tensor(cy_r[u % 2], hs_r[u % 2], cwide[:, 0:CH], ALU.mult
                                            ).then_inc(cy_ready, 1)
                u = v - 2
                if 0 <= u < UNITS:
                    done = UNITS * i + u
                    dve.wait_ge(bu_ready, done + 1)
                    dve.wait_ge(z_ready, done + 1)
                    nc.vector.tensor_tensor(v_r[u % 3], z_r[u % 2], v_r[u % 3], ALU.mult).then_inc(scaled, 1)
                u = v - 3
                if 0 <= u < UNITS:
                    c, p = divmod(u, PAIRS)
                    done = UNITS * i + u
                    dve.wait_ge(scaled, done + 1)
                    dve.wait_ge(lam_ready, done + 1)
                    start = 0.0
                    if c:
                        start = carry[:, p:p + 1]
                        dve.wait_ge(carried, UNITS * i + u - PAIRS + 1)
                    ring_free(dve, cy_ready, done - 1)
                    nc.vector.tensor_tensor_scan(hs_r[u % 2], lam_r[u % 3], v_r[u % 3], start,
                                                 ALU.mult, ALU.add).then_inc(scanned, 1)

            def chunk(kind, b, i, c):
                dve.wait_ge(y_summed, UNITS * i + (c + 1) * PAIRS)
                cols = slice(c * CH, (c + 1) * CH)
                nc.vector.tensor_tensor(gy, gate[:, cols], ysum[DIM:P, 0:CH], ALU.mult).then_inc(gated, 1)
                dve.wait_ge(small_filled.sem, small_filled.after(kind, b, ("out", c)))
                nc.vector.tensor_tensor(h_t[:, cols], h_t[:, cols], small[0:DIM, 0:CH], ALU.add
                                        ).then_inc(small_drained.sem, 1)

            def rank(kind, b, t, g, piece):
                first = RANK_STEPS * g + RANK_AT[piece]
                count = [0]

                def after(ins):
                    count[0] += 1
                    ins.then_inc(rank_step, 1)
                    dve.wait_ge(rank_step, first + count[0])
                    plain(dve)

                RANK_PIECES[piece](kind, b, t, g, after)
                assert count[0] == RANK_AT[piece + 1] - RANK_AT[piece], (piece, count)

            groups = range(2 * HEADS)

            def first_eight(kind, b, t, g, after):
                dve.wait_ge(wide_drained.sem, wide_drained.after(kind, b, None if kind != "first" and t == 1 else ("sim", t)))
                plain(dve)
                for q in groups:
                    last = nc.vector.max(top_v[:, q, 0:8], sims[:, q, :])
                after(last)
                for q in groups:
                    nc.vector.max_index(top_i[:, q, 0:8], top_v[:, q, 0:8], sims[:, q, :])
                for q in groups:
                    last = nc.vector.match_replace(sims[:, q, :], top_v[:, q, 0:8], sims[:, q, :], LOWEST)
                after(last)

            def pairs(dst, first, second):
                for a in range(5):
                    m, o = LIMITS[a], PLACES[a]
                    nc.vector.tensor_tensor(dst[:, :, o:o + m], second[:, :, 0:m],
                                            first[:, :, a:a + 1].broadcast_to([P, HEADS, m]), ALU.add)
                o = PLACES[5]
                nc.vector.tensor_tensor(
                    dst[:, :, o:o + 6].rearrange("p h (a c) -> p h a c", c=2),
                    second[:, :, 0:2].unsqueeze(2).broadcast_to([P, HEADS, 3, 2]),
                    first[:, :, 5:8].unsqueeze(3).broadcast_to([P, HEADS, 3, 2]), ALU.add)
                return nc.vector.tensor_tensor(dst[:, :, PLACES[8]:], first[:, :, 8:],
                                               second[:, :, 0:1].broadcast_to([P, HEADS, 8]), ALU.add)

            def next_eight(kind, b, t, g, after):
                for q in groups:
                    last = nc.vector.max(top_v[:, q, 8:16], sims[:, q, :])
                after(last)
                for q in groups:
                    last = nc.vector.max_index(top_i[:, q, 8:16], top_v[:, q, 8:16], sims[:, q, :])
                after(last)
                after(nc.vector.tensor_scalar(idx1[:], top_i[:, HEADS:, :], float(KEYS), None, ALU.mult))
                pairs(cand[:], top_v[:, 0:HEADS, :], top_v[:, HEADS:, :])
                after(pairs(cand_i[:], top_i[:, 0:HEADS, :], idx1[:]))

            def best_pairs(kind, b, t, g, after):
                for h in range(HEADS):
                    last = nc.vector.max(best[:, h, 0:8], cand[:, h, :])
                after(last)
                for h in range(HEADS):
                    nc.vector.max_index(best_at[:, h, 0:8], best[:, h, 0:8], cand[:, h, :])
                for h in range(HEADS):
                    last = nc.vector.match_replace(cand[:, h, :], best[:, h, 0:8], cand[:, h, :], LOWEST)
                after(last)
                for h in range(HEADS):
                    last = nc.vector.max(best[:, h, 8:16], cand[:, h, :])
                after(last)
                for h in range(HEADS):
                    last = nc.vector.max_index(best_at[:, h, 8:16], best[:, h, 8:16], cand[:, h, :])
                after(last)
                ring_free(dve, weight_ready, g)
                after(nc.vector.tensor_copy(zinv[:], best[:, :, 0]))
                nc.vector.tensor_tensor(best[:], best[:], zinv[:].unsqueeze(2).broadcast_to([P, HEADS, TOP]),
                                        ALU.subtract).then_inc(shifted, 1)

            def row_numbers(ks, after):
                for k in ks:
                    two = slice(2 * k, 2 * k + 2)
                    shape = [P, 2, TOP, CANDS]
                    after(nc.vector.tensor_tensor(
                        hot[:], best_at[:, two, :].unsqueeze(3).broadcast_to(shape),
                        place[:].unsqueeze(1).unsqueeze(1).broadcast_to(shape), ALU.is_equal))
                    after(nc.vector.tensor_tensor(
                        hot[:], hot[:], cand_i[:, two, :].unsqueeze(2).broadcast_to(shape), ALU.mult))
                    after(nc.vector.tensor_reduce(row_f[:, two, :], hot[:], AX.X, ALU.add))

            def rows_0(kind, b, t, g, after):
                row_numbers((0,), after)

            def rows_1(kind, b, t, g, after):
                row_numbers((1, 2), after)

            def rows_2(kind, b, t, g, after):
                row_numbers((3,), after)
                nc.vector.tensor_tensor(row_i[:, t % 3, :].rearrange("p (h j) -> p h j", j=TOP), row_f[:],
                                        head_base[:].unsqueeze(2).broadcast_to([P, HEADS, TOP]), ALU.add
                                        ).then_inc(row_i_ready, 1)

            def softmax(kind, b, t, g, after):
                dve.wait_ge(expo_ready, g + 1)
                after(nc.vector.tensor_reduce(zsum[:], expo[:], AX.X, ALU.add))
                after(nc.vector.reciprocal(zinv[:], zsum[:]))
                nc.vector.tensor_tensor(weight[:, t % 3, :, :], expo[:],
                                        zinv[:].unsqueeze(2).broadcast_to([P, HEADS, TOP]), ALU.mult
                                        ).then_inc(weight_ready, 1)

            RANK_PIECES = (first_eight, next_eight, best_pairs, rows_0, rows_1, rows_2, softmax)
            RANK_AT = (0, 2, 6, 11, 14, 20, 23, 25)
            assert RANK_AT[-1] == RANK_STEPS

            def step(kind, b, t, s, ticks):
                g = TILES * b + t

                def scan(k):
                    if k < len(ticks):
                        tick(*tick_batch(b, ticks[k]))

                def weigh(h):
                    dve.wait_ge(weight_ready, g + 1)
                    dve.wait_ge(gathered[h], 16 * TOP * (g + 1))
                    nc.vector.tensor_tensor(rows[:, h, :, :], rows[:, h, :, :],
                                            weight[:, t % 3, h, :].unsqueeze(2).broadcast_to([P, TOP, ROW]),
                                            ALU.mult).then_inc(weighted, 1)
                    dve.wait_ge(weighted, HEADS * g + h + 1)
                    nc.vector.tensor_tensor(rows[:, h, 0:FOLDED, :], rows[:, h, 0:FOLDED, :],
                                            rows[:, h, FOLDED:TOP, :], ALU.add).then_inc(halved, 1)

                ranking = s < 4 and (kind == "turn" or t + 1 < TILES)
                if s:
                    row_max(kind, b, t, 2 * s - 2)
                scan(0)
                if s < HEADS // 2:
                    weigh(2 * s)
                scan(1)
                if s < HEADS // 2:
                    weigh(2 * s + 1)
                if ranking:
                    rank(kind, b, t + 1, g + 1, 2 * s)
                if s:
                    row_max(kind, b, t, 2 * s - 1)
                scan(2)
                if ranking and s < 3:
                    rank(kind, b, t + 1, g + 1, 2 * s + 1)
                scan(3)

            def row_max(kind, b, t, h):
                full(kind, b, ("score", t, h))
                nc.vector.tensor_reduce(nmax[:, h:h + 1], wide_flat[:, 0:(t + 1) * P], AX.X, ALU.max,
                                        negate=True).then_inc(max_ready, 1)

            def finish(g):
                dve.wait_ge(o_filled, g + 1)
                dve.wait_ge(o_normed, g + CREDIT)
                nc.vector.reciprocal(rinv[:], rsum[:]).then_inc(o_inv, 1)
                dve.wait_ge(o_inv, g + 1)
                nc.vector.tensor_tensor(o_n[:], attn[:].rearrange("p (h d) -> p h d", d=DIM),
                                        rinv[:].unsqueeze(2).broadcast_to([P, HEADS, DIM]), ALU.mult
                                        ).then_inc(o_normed, 1)

            def close(g, t):
                dve.wait_ge(fin_filled, g + 1)
                dve.wait_ge(stored, 16 * (g + CREDIT))
                nc.vector.tensor_tensor(out_s[:], res[:, t % 3, :], attn[:, 0:DIM], ALU.add).then_inc(out_ready, 1)

            def turn(kind, b):
                for name, a, n in stages(kind):
                    i = b if kind == "first" or name == "norm" and a else b + 1
                    if name == "front":
                        front(kind, b, i, a)
                    elif name == "ticks":
                        for v in n:
                            tick(0, v)
                    elif name == "norm":
                        chunk(kind, b, i, a)
                        cols = norm_parts(a)[2]
                        layer_norm(kind, b, i, a, xn_t[:, cols])
                    elif name == "rank":
                        for piece in (2 * n, 2 * n + 1)[:1 + (n < 3)]:
                            rank(kind, b, a, a, piece)
                    elif name == "step":
                        step(kind, b, a, *n)
                    elif name == "finish":
                        finish(TILES * b + a)
                    elif name == "close":
                        close(TILES * b + a, a)

            dve.sem_inc(o_normed, CREDIT)
            dve.sem_inc(out_ready, CREDIT)
            turn("first", 0)
            with dve.Fori(0, BATCH - 1) as b:
                turn("turn", b)
            turn("last", BATCH - 1)

        @block.tensor
        def _(pe):
            pe.wait_ge(weights_in, 16 * len(loads))
            for o in range(DIM):
                for late in range(2):
                    dst = wide_flat[CHANNELS * late:CHANNELS * late + CHANNELS, 0:512]
                    mm = nc.tensor.matmul(dst.rearrange("p (k o) -> p k o", o=DIM)[:, :, o], w18[:, o, :],
                                          dft_s[:, STRIDE * late:STRIDE * late + STRIDE], start=True, stop=True)
            mm.then_inc(wide_filled.sem, 1)
            pe.wait_ge(wide_drained.sem, wide_drained.after("first", 0, "weff"))
            for q in range(2 * HEADS):
                mm = nc.tensor.matmul(wide_flat[0:DIM, q * KEYS:(q + 1) * KEYS], wqpk_s[:, q, :], keys_s[:, q, :],
                                      start=True, stop=True)
            mm.then_inc(wide_filled.sem, 1)
            pe.wait_ge(set_up, SETUP_STEPS)

            def free_wide(kind, b, key):
                pe.wait_ge(wide_drained.sem, wide_drained.before(kind, b, key))
                plain(pe)

            def free_small(kind, b, key):
                pe.wait_ge(small_drained.sem, small_drained.before(kind, b, key))
                plain(pe)

            def over_chunks(kind, b, key, parts, lhs, rhs):
                free_wide(kind, b, key)
                for c in range(rhs.shape[1] // CH):
                    mm = nc.tensor.matmul(wide[parts, c, 0:CH], lhs, rhs[:, c * CH:(c + 1) * CH],
                                          start=True, stop=True)
                mm.then_inc(wide_filled.sem, 1)

            def layer_norm(kind, b, i, c):
                (mean, var), (_, sq, _, _), cols, _ = norm_parts(c)
                for key, src in ((mean, h_t[:, cols]), (var, sq)):
                    if key == var:
                        pe.wait_ge(squared, norm_of(i, c) + 1)
                    over_chunks(kind, b, key, slice(0, DIM), mean_w[:], src)

            def front(kind, b, i, part):
                if part < 2:
                    pe.wait_ge(x_in[part], (32 + 16 * part) * (i + 1))
                    free_wide(kind, b, f"tok{part}")
                    for k in range(STRIDE):
                        mm = nc.tensor.matmul(wide[0:DIM, 0, :], w_eff[:, k, :], x2[:, k:64:STRIDE, :],
                                              start=(k == 0), stop=(k == STRIDE - 1))
                    mm.then_inc(wide_filled.sem, 1)
                if part == 1:
                    pe.wait_ge(wide_drained.sem, wide_drained.after(kind, b, "tok1"))
                    pe.wait_ge(text_in, 16 * (i + 1))
                    layer_norm(kind, b, i, None)
                if part < 2:
                    return
                pe.wait_ge(normed, norm_of(i, None) + 1)
                over_chunks(kind, b, "skip", slice(DIM, P), win[:, 0, :], x_c)
                over_chunks(kind, b, "u", slice(0, P), win[:, 1:3, :], x_c)
                pe.wait_ge(convolved, TAPS * i + TAPS)
                over_chunks(kind, b, "bc", slice(0, P), wbc[:], u_t[0:DIM, :])
                over_chunks(kind, b, "lam", slice(0, P), wlam[:], u_t[0:DIM, :])
                pe.wait_ge(wide_drained.sem, wide_drained.after(kind, b, "bc"))

            def spread_state(dst, rows, u, c):
                return nc.tensor.matmul(dst[:, 0:CH], pick[u % PICKS][rows, :, :].rearrange("p a b -> p (a b)"),
                                        bc_t[rows, c * CH:(c + 1) * CH], start=True, stop=True)

            def tick(i, v):
                if v < UNITS:
                    ring_free(pe, bu_ready, UNITS * i + v)
                    pe.wait_ge(picked, UNITS * i + v + 1)
                    plain(pe)
                    spread_state(bwide, slice(0, STATE), v, v // PAIRS).then_inc(b_ready, 1)
                u = v - 3
                if 0 <= u < UNITS:
                    ring_free(pe, cy_ready, UNITS * i + u)
                    plain(pe)
                    spread_state(cwide, slice(STATE, P), u, u // PAIRS).then_inc(c_ready, 1)
                u = v - LAG
                if u >= 0:
                    c, p = divmod(u, PAIRS)
                    pe.wait_ge(cy_ready, UNITS * i + u + 1)
                    if p == 0:
                        ring_free(pe, gated, CHUNKS * i + c)
                    nc.tensor.matmul(ysum[DIM:P, 0:CH], fold[:], cy_r[u % 2], start=(p == 0),
                                     stop=(p == PAIRS - 1)).then_inc(y_summed, 1)

            def chunk(kind, b, i, c):
                pe.wait_ge(gated, CHUNKS * i + c + 1)
                free_small(kind, b, ("out", c))
                nc.tensor.matmul(small[0:DIM, 0:CH], wout, gy, start=True, stop=True
                                 ).then_inc(small_filled.sem, 1)

            def norm(kind, b, i, c):
                chunk(kind, b, i, c)
                pe.wait_ge(small_drained.sem, small_drained.after(kind, b, ("out", c)))
                layer_norm(kind, b, i, c)

            def query(kind, b, t):
                pe.wait_ge(normed, norm_of(b, t // 3) + 1)
                free_small(kind, b, ("q", t))
                tile = slice(t * P, (t + 1) * P)
                for hp in range(HEADS // 2):
                    mm = nc.tensor.matmul(small[:, hp * P:(hp + 1) * P], wq[:, hp * P:(hp + 1) * P],
                                          xn_t[:, tile], start=True, stop=True)
                mm.then_inc(small_filled.sem, 1)
                pe.wait_ge(h1_copied, CHUNKS * b + t // 3 + 1)
                free_small(kind, b, ("res", t))
                nc.tensor.transpose(small[:, 0:DIM], h1_t[:, tile], ident[DIM:P, DIM:P]
                                    ).then_inc(small_filled.sem, 1)

            def sim(kind, b, t, i):
                pe.wait_ge(normed, norm_of(i, t % TILES // 3) + 1)
                free_wide(kind, b, ("sim", t))
                for n in range(2):
                    mm = nc.tensor.matmul(wide[:, n, :], xn_t[:, (t % TILES) * P:(t % TILES + 1) * P],
                                          wcomb[:, n * 512:(n + 1) * 512], start=True, stop=True)
                mm.then_inc(wide_filled.sem, 1)

            def scores(kind, b, t, h):
                hp, half = h // 2, DIM * (h % 2)
                free_wide(kind, b, ("score", t, h))
                n = (t + 1) * P
                for lo in range(0, n, 512):
                    hi = min(lo + 512, n)
                    mm = nc.tensor.matmul(wide_flat[:, lo:hi], q_t[half:half + DIM, hp, :],
                                          k_t[half:half + DIM, hp, lo:hi], start=True, stop=(hi < n))
                nc.tensor.matmul(wide_flat[:, n - P:n], ident[:], causal[:], start=False, stop=True
                                 ).then_inc(wide_filled.sem, 1)

            def turned(kind, b, t, h):
                free_wide(kind, b, ("turned", t, h))
                for j in range(t + 1):
                    mm = nc.tensor.transpose(wide_flat[:, j * P:(j + 1) * P], prob[:, j * P:(j + 1) * P], ident[:])
                mm.then_inc(wide_filled.sem, 1)

            def attend(kind, b, t, h):
                pe.wait_ge(wide_drained.sem, wide_drained.after(kind, b, ("turned", t, h)))
                if h == 0:
                    pe.wait_ge(out_ready, TILES * b + t + CREDIT)
                for j in range(t + 1):
                    mm = nc.tensor.matmul(attn[:, h * DIM:(h + 1) * DIM], prob_t[:, j * P:(j + 1) * P],
                                          vals[:, j, h, :], start=(j == 0), stop=(j == t))
                if h == HEADS - 1:
                    mm.then_inc(o_filled, 1)

            def row_sum(kind, b, t, h):
                pe.wait_ge(halved, HEADS * (TILES * b + t) + h + 1)
                free_small(kind, b, ("kv", t, h))
                for j in range(FOLDED):
                    mm = nc.tensor.matmul(small[:, 0:ROW], ident[:], rows[:, h, j, :], start=(j == 0),
                                          stop=(j == FOLDED - 1))
                mm.then_inc(rows_summed[h], 1)

            def step(kind, b, t, s, ticks):
                old, new = (2 * s - 2, 2 * s - 1), (2 * s, 2 * s + 1)
                attending, summing = s > 0, s < HEADS // 2

                def scan(k):
                    if k < len(ticks):
                        tick(*tick_batch(b, ticks[k]))

                if attending:
                    pe.wait_ge(small_drained.sem, small_drained.after(kind, b, ("keys", t, s - 1)))
                    scores(kind, b, t, old[0])
                scan(0)
                if attending:
                    turned(kind, b, t, old[0])
                if summing:
                    row_sum(kind, b, t, new[0])
                if attending:
                    scores(kind, b, t, old[1])
                scan(1)
                if attending:
                    attend(kind, b, t, old[0])
                if summing:
                    row_sum(kind, b, t, new[1])
                    free_small(kind, b, ("keys", t, s))
                    nc.tensor.transpose(small[:, 0:P], k_nat[:].rearrange("p h d -> p (h d)"), ident[:]
                                        ).then_inc(small_filled.sem, 1)
                if attending:
                    turned(kind, b, t, old[1])
                scan(2)
                scan(3)
                if attending:
                    attend(kind, b, t, old[1])

            def finish(g):
                pe.wait_ge(o_normed, g + 1 + CREDIT)
                for c in range(HEADS // 2):
                    mm = nc.tensor.transpose(attn[:, c * P:(c + 1) * P],
                                             o_n[:].rearrange("p h d -> p (h d)")[:, c * P:(c + 1) * P], ident[:])
                mm.then_inc(o_turned, 1)
                pe.wait_ge(o_t_ready, g + 1)
                for c in range(HEADS // 2):
                    mm = nc.tensor.matmul(attn[:, 0:DIM], o_t[:, c, :], wo[:, c, :], start=(c == 0),
                                          stop=(c == HEADS // 2 - 1))
                mm.then_inc(fin_filled, 1)

            def turn(kind, b):
                for name, a, n in stages(kind):
                    i = b if kind == "first" or name == "norm" and a else b + 1
                    if name == "front":
                        front(kind, b, i, a)
                    elif name == "ticks":
                        for v in n:
                            tick(0, v)
                    elif name == "norm":
                        norm(kind, b, i, a)
                    elif name == "query":
                        query(kind, b, a)
                    elif name == "sim":
                        sim(kind, b, a, b + a // TILES)
                    elif name == "step":
                        step(kind, b, a, *n)
                    elif name == "finish":
                        finish(TILES * b + a)

            for h in range(HEADS):
                pe.sem_inc(rows_summed[h], CREDIT)
            turn("first", 0)
            with pe.Fori(0, BATCH - 1) as b:
                turn("turn", b)
            turn("last", BATCH - 1)


EXP_AND_LN = "natural_log_exp_and_others"
SERIES = (17, 15, 13, 11, 9, 7, 5, 3)
SETUP_STEPS = 12 + len(SERIES)


def dft_table():
    angle = 2 * np.pi * np.arange(FREQS)[:, None] * np.arange(PATCH)[None, :] / PATCH
    return (np.concatenate([np.cos(angle), -np.sin(angle)]) / np.sqrt(PATCH)).astype(np.float32)


def kernel(**inputs):
    import concourse.bacc as bacc
    from concourse.bass_utils import run_bass_kernel_spmd

    a = {k: np.asarray(v) for k, v in inputs.items()}
    col = lambda v: v.reshape(-1, 1)
    arrays = {
        "x": a["x"],
        "text": a["txt"],
        "text_t": a["txt"].transpose(0, 2, 1),
        "w_tok": a["L0_tok_W"].reshape(DIM, 2 * FREQS, CHANNELS).transpose(1, 0, 2),
        "dft": dft_table(),
        "w_in": a["L0_attn_W_in"].T,
        "conv_w": a["L0_attn_conv_w"].reshape(DIM, TAPS),
        "conv_b": col(a["L0_attn_conv_b"]),
        "w_bc": a["L0_attn_W_bc"].T,
        "b_bc": col(a["L0_attn_b_bc"]),
        "w_lam": a["L0_attn_W_lam"].T,
        "b_lam": col(a["L0_attn_b_lam"]),
        "decay": a["L0_attn_A"].reshape(PAIRS, 2, DIM).transpose(1, 2, 0).reshape(P, PAIRS),
        "w_out": a["L0_attn_W_out"].T,
        "w_qpk": a["L0_ffn_Wq_pk"].reshape(DIM, 2 * HEADS, KEYDIM).transpose(2, 1, 0),
        "keys": a["L0_ffn_pk_keys"].transpose(3, 0, 2, 1).reshape(KEYDIM, 2 * HEADS, KEYS),
        "w_q": a["L0_ffn_Wq"],
        "tables": np.concatenate([a["L0_ffn_keys_table"], a["L0_ffn_values_table"]], axis=1),
        "w_o": a["L0_ffn_Wo"].reshape(HEADS * DIM // P, P, DIM).transpose(1, 0, 2),
        "ident_d": np.eye(P, dtype=np.float32),
        "fold_d": np.tile(np.eye(DIM, dtype=np.float32), (2, 1)),
        "causal_d": np.triu(np.full((P, P), MASKED, np.float32), 1),
    }
    nc = bacc.Bacc("TRN2", target_bir_lowering=False, num_devices=1)
    arrays = {f"in_{k}": np.ascontiguousarray(v) for k, v in arrays.items()}
    args = {k[3:]: nc.dram_tensor(k, v.shape, mybir.dt.from_np(v.dtype), kind="ExternalInput").ap()
            for k, v in arrays.items()}
    args["out"] = nc.dram_tensor("out", (BATCH, LEN, DIM), F32, kind="ExternalOutput").ap()
    program(nc, **args)
    r = run_bass_kernel_spmd(nc, [arrays], core_ids=[0])
    return r.results[0]["out"]
```

```python
from contextlib import ExitStack

import numpy as np

import concourse.bass as bass
from concourse import mybir

F32 = mybir.dt.float32
BF16 = mybir.dt.bfloat16
U32 = mybir.dt.uint32
ALU = mybir.AluOpType
ACT = mybir.ActivationFunctionType
AX = mybir.AxisListType

P = 128
BATCH, CHANNELS, TIME, VARS = 4, 64, 128, 64
PATCH, STRIDE = 16, 8
PATCHES = TIME // STRIDE
FREQS = PATCH // 2 + 1
DIM = 64
TEXT = 128
TOKENS = VARS * PATCHES
LEN = TOKENS + TEXT
TILES = LEN // P
STATE = 64
TAPS = 4
PAIRS = STATE // 2
CHUNKS = 3
CH = LEN // CHUNKS
UNITS = CHUNKS * PAIRS
LAG = 4
HEAD_TICKS = PAIRS + LAG
SCAN_TICKS = UNITS + 2 * LAG
HEADS = 8
KEYS = 64
TOP = 16
FOLDED = TOP // 2
KEYDIM = 32
ROW = 2 * DIM
LIMITS = [TOP // (a + 1) for a in range(TOP)]
PLACES = [sum(LIMITS[:a]) for a in range(TOP)]
CANDS = sum(LIMITS)
LOWEST = float(np.finfo(np.float32).min)
MASKED = -1e30
LN_EPS = 1e-5
DECAY_EPS = 1e-6
NORMS = [("in", 0), ("out", 0), ("in", 1), ("in", 2), ("out", 1), ("out", 2)]
PARTS = 3
PICKS = 4
CREDIT = 2
RANK_STEPS = 25

TICKS = ((5, 5, 5, 4), (6, 6, 5, 0), (4, 4, 4, 4), (4, 4, 4, 4), (0, 0, 0, 0),
         (0, 4, 4, 4), (4, 4, 4, 3), (3, 3, 3, 0), (0, 0, 0, 0))
FOLLOWING = {
    (0, 1): [("front", 2, 0)], (0, 2): [("front", 2, 1)], (0, 3): [("front", 2, 2)], (1, 0): [("front", 2, 3)],
    (1, 2): [("out", 1, 0)], (1, 3): [("out", 1, 1), ("out", 1, 2)],
    (3, 3): [("out", 2, 0)], (4, 0): [("out", 2, 1), ("out", 2, 2)],
    (4, 1): [("tok", 0, 0)], (4, 2): [("tok", 1, 0)], (4, 3): [("front", 0, 0), ("front", 0, 1)],
    (5, 0): [("front", 0, 2), ("front", 0, 3)],
    (7, 2): [("out", 0, 0)], (7, 3): [("out", 0, 1), ("out", 0, 2)],
    (8, 0): [("front", 1, 0)], (8, 1): [("front", 1, 1)], (8, 2): [("front", 1, 2)], (8, 3): [("front", 1, 3)],
}
OWN = (("front", 2), ("out", 1), ("out", 2))


def attended(t, s):
    if s:
        return t, s - 1
    return (t - 1, HEADS // 2 - 1) if t else None


def stages(kind):
    if kind == "first":
        for half in range(2):
            yield "tok", half, 0
        for part in range(4):
            yield "front", 0, part
        yield "keys", 0, 0
        yield "ticks", 0, range(HEAD_TICKS)
        for part in range(3):
            yield "out", 0, part
        yield "sim", 0, 0
        for s in range(4):
            yield "rank", 0, s
        yield "sim", 1, 0
        for part in range(4):
            yield "front", 1, part
        yield "step", 0, (0, range(HEAD_TICKS, HEAD_TICKS + TICKS[0][0]))
        yield "query", 0, 0
        return
    ahead = kind == "turn"
    tick = HEAD_TICKS + TICKS[0][0]
    for t in range(TILES):
        for s in range(t == 0, HEADS // 2):
            n = TICKS[t][s] if ahead or tick < SCAN_TICKS else 0
            yield "step", t, (s, range(tick, tick + n))
            tick += n
            if s == 0:
                yield "finish", t - 1, 0
                yield "query", t, 0
            for stage in FOLLOWING.get((t, s), ()):
                if ahead or stage[:2] in OWN:
                    yield stage
        if ahead or t + 2 < TILES:
            yield "sim", t + 2, 0
    if ahead:
        yield "step", TILES, (0, range(tick, tick + TICKS[0][0]))
    else:
        yield "step", TILES - 1, (HEADS // 2, range(0))
    yield "finish", TILES - 1, 0
    if ahead:
        yield "query", TILES, 0
    yield "close", TILES - 1, 0


def wide_steps(kind):
    out = ["weff"] if kind == "first" else []
    for name, a, s in stages(kind):
        if name == "keys":
            out += ["wcomb"]
        elif name == "tok":
            out += [("tok", a)]
        elif name == "front":
            out += [("in", a, ("mean", "var", "proj", "gates")[s])]
        elif name == "out" and s:
            out += [("out", a, ("mean", "var")[s - 1])]
        elif name == "sim":
            out += [("sim", a)]
        elif name == "step" and attended(a, s[0]):
            t, pair = attended(a, s[0])
            out += [(what, t, h) for h in (2 * pair, 2 * pair + 1) for what in ("score", "turned")]
    return out


def small_steps(kind, filled):
    out = []
    for name, a, s in stages(kind):
        if name == "query":
            out += [("q", a), ("res", a)]
        elif name == "out" and s == 0:
            out += [("out", a)]
        elif name == "step" and s[0] < HEADS // 2:
            s = s[0]
            out += [] if filled else [("kv", a, 2 * s), ("kv", a, 2 * s + 1)]
            out += [("keys", a, s)]
    return out


class Count:

    def __init__(self, sem, lists):
        self.sem = sem
        self.at = {kind: {key: i for i, key in enumerate(steps)} for kind, steps in lists.items()}
        self.first, self.turn = len(lists["first"]), len(lists["turn"])

    def before(self, kind, b, key):
        i = self.at[kind][key]
        return i if kind == "first" else b * self.turn + (self.first + i)

    def after(self, kind, b, key):
        i = self.at[kind][key] + 1 if key else 0
        return i if kind == "first" else b * self.turn + (self.first + i)


def program(nc, x, text, text_t, w_tok, dft, w_in, conv_w, conv_b, w_bc, b_bc, w_lam, b_lam, decay, w_out,
            w_qpk, keys, w_q, tables, w_o, ident_d, fold_d, causal_d, out):
    kinds = ("first", "turn", "last")
    with ExitStack() as ctx:
        def sb(name, shape, dt=F32):
            return ctx.enter_context(nc.sbuf_tensor(name, shape, dt))

        def ps(name, shape):
            return ctx.enter_context(nc.psum_tensor(name, shape, F32))

        def sem(name):
            return ctx.enter_context(nc.semaphore(name))

        wide = ps("wide", [P, 3, 512])
        small = ps("small", [P, 512])
        attn = ps("attn", [P, 512])
        bwide = ps("bwide", [P, 512])
        cwide = ps("cwide", [P, 512])
        ysum = ps("ysum", [P, 512])
        wide_flat = wide[:].rearrange("p a b -> p (a b)")

        ident = sb("ident", [P, P])
        fold = sb("fold", [P, DIM])
        causal = sb("causal", [P, P])
        dft_s = sb("dft_s", [2 * FREQS, PATCH])
        mean_w = sb("mean_w", [DIM, DIM])
        one_eps = sb("one_eps", [P, 1])
        ln_eps = sb("ln_eps", [P, 1])
        w_eff = sb("w_eff", [P, STRIDE, DIM])
        win = sb("win", [DIM, 3, DIM])
        cw = sb("cw", [P, TAPS])
        cb = sb("cb", [P, 1])
        wbc = sb("wbc", [DIM, P])
        bbc = sb("bbc", [P, 1])
        wlam = sb("wlam", [DIM, 2, DIM])
        blam = sb("blam", [P, 1])
        nblam = sb("nblam", [P, 1])
        wout = sb("wout", [P, DIM])[DIM:P, :]
        coef = sb("coef", [P, PAIRS])
        coef2 = sb("coef2", [P, PAIRS])
        wcomb = sb("wcomb", [DIM, 2 * HEADS * KEYS])
        wq = sb("wq", [DIM, HEADS * DIM])
        wo = sb("wo", [P, HEADS * DIM // P, DIM])
        head_base = sb("head_base", [P, HEADS], U32)
        place = sb("place", [P, CANDS], U32)

        h_both = sb("h_both", [P, LEN])
        h_t, h1_t = h_both[0:DIM, :], h_both[DIM:P, :]
        upad = sb("upad", [P, LEN + TAPS - 1])
        x_c = upad[0:DIM, TAPS - 1:]
        bc_f = sb("bc_f", [P, CH])
        bc_t = sb("bc_t", [P, PARTS, LEN], BF16)
        u_t = sb("u_t", [P, LEN])
        sig = sb("sig", [P, LEN])
        xn_gate = sb("xn_gate", [P, LEN])
        xn_t, gate = xn_gate[0:DIM, :], xn_gate[DIM:P, :]
        carry = sb("carry", [P, PAIRS])
        gy = sb("gy", [P, CH])[DIM:P, :]
        arena = sb("arena", [P, 12 * CH])
        x2 = arena[:, 0:64 * VARS].rearrange("p (t v) -> p t v", v=VARS)

        def ring(first, n):
            return [arena[:, (first + i) * CH:(first + i + 1) * CH] for i in range(n)]

        lam_r, v_r, z_r, hs_r, cy_r = ring(0, 3), ring(3, 3), ring(6, 2), ring(8, 2), ring(10, 2)
        xc, sq, rr = (sb(name, [DIM, CH])[:] for name in ("xc", "sq", "rr"))
        pick = [sb(f"pick{i}", [P, 2, DIM], BF16) for i in range(PICKS)]

        sims = sb("sims", [P, 2 * HEADS, KEYS])
        top_v = sb("top_v", [P, 2 * HEADS, TOP])
        top_i = sb("top_i", [P, 2 * HEADS, TOP], U32)
        idx1 = sb("idx1", [P, HEADS, TOP])
        cand = sb("cand", [P, HEADS, CANDS])
        cand_i = sb("cand_i", [P, HEADS, CANDS])
        best = sb("best", [P, HEADS, TOP])
        best_at = sb("best_at", [P, HEADS, TOP], U32)
        hot = sb("hot", [P, 2, TOP, CANDS])
        row_f = sb("row_f", [P, HEADS, TOP])
        expo = sb("expo", [P, HEADS, TOP])
        zsum = sb("zsum", [P, HEADS])
        zinv = sb("zinv", [P, HEADS])
        row_i = sb("row_i", [P, 3, HEADS * TOP], U32)
        weight = sb("weight", [P, 3, HEADS, TOP])

        rows = sb("rows", [P, HEADS, TOP, ROW])
        vals = sb("vals", [P, TILES, HEADS, DIM])
        k_nat = sb("k_nat", [P, 2, DIM])
        k_t = sb("k_t", [P, HEADS // 2, LEN])
        q_t = sb("q_t", [P, HEADS // 2, P])
        res = sb("res", [P, 3, DIM])
        nmax = sb("nmax", [P, HEADS])
        rsum = sb("rsum", [P, HEADS])
        rinv = sb("rinv", [P, HEADS])
        prob = sb("prob", [P, LEN])
        prob_t = sb("prob_t", [P, LEN])
        o_n = sb("o_n", [P, HEADS, DIM])
        o_t = sb("o_t", [P, HEADS * DIM // P, P])
        out_s = sb("out_s", [P, DIM])

        rows_flat = rows[:].rearrange("p h j r -> p (h j r)")
        w18 = rows_flat[0:2 * FREQS, 0:DIM * CHANNELS].rearrange("r (o c) -> r o c", o=DIM)
        wqpk_s = rows_flat[0:KEYDIM, 4096:5120].rearrange("d (g i) -> d g i", i=DIM)
        keys_s = rows_flat[0:KEYDIM, 5120:6144].rearrange("d (g k) -> d g k", k=KEYS)

        x2_late = rows_flat[:, 8192:8192 + 64 * VARS].rearrange("p (t v) -> p t v", v=VARS)

        def x_place(kind, half):
            return x2_late if kind == "first" and half else x2

        raw_a, *sp = [rows_flat[:, 6144 + i * PAIRS:6144 + (i + 1) * PAIRS] for i in range(5)]

        fourier_in = sem("fourier_in")
        weights_in = sem("weights_in")
        passed = sem("passed")
        set_up = sem("set_up")
        spread = sem("spread")
        pos_ready = sem("pos_ready")
        x_in = [sem("x_in0"), sem("x_in1")]
        text_in = sem("text_in")
        wide_filled = Count(sem("wide_filled"), {k: wide_steps(k) for k in kinds})
        wide_drained = Count(sem("wide_drained"), {k: wide_steps(k) for k in kinds})
        small_filled = Count(sem("small_filled"), {k: small_steps(k, True) for k in kinds})
        small_drained = Count(sem("small_drained"), {k: small_steps(k, False) for k in kinds})
        squared = sem("squared")
        log_ready = sem("log_ready")
        inv_ready = sem("inv_ready")
        newton = sem("newton")
        normed = sem("normed")
        convolved = sem("convolved")
        u_copied = sem("u_copied")
        sig_exp = sem("sig_exp")
        bc_rounded = sem("bc_rounded")
        bc_rest = sem("bc_rest")
        sig_step = sem("sig_step")
        lam_ready = sem("lam_ready")
        lam2_ready = sem("lam2_ready")
        z_log = sem("z_log")
        picked = sem("picked")
        z_ready = sem("z_ready")
        b_ready = sem("b_ready")
        c_ready = sem("c_ready")
        bu_ready = sem("bu_ready")
        scaled = sem("scaled")
        scanned = sem("scanned")
        carried = sem("carried")
        cy_ready = sem("cy_ready")
        y_summed = sem("y_summed")
        gated = sem("gated")
        h1_copied = sem("h1_copied")
        rank_step = sem("rank_step")
        shifted = sem("shifted")
        expo_ready = sem("expo_ready")
        row_i_ready = sem("row_i_ready")
        weight_ready = sem("weight_ready")
        gathered = [sem(f"gathered{h}") for h in range(HEADS)]
        weighted_even = sem("weighted_even")
        weighted_odd = sem("weighted_odd")
        halved = sem("halved")
        rows_summed = [sem(f"rows_summed{h}") for h in range(HEADS)]
        max_ready = sem("max_ready")
        o_filled = sem("o_filled")
        o_inv = sem("o_inv")
        o_normed = sem("o_normed")
        o_turned = sem("o_turned")
        o_t_ready = sem("o_t_ready")
        fin_filled = sem("fin_filled")
        out_ready = sem("out_ready")
        stored = sem("stored")

        loads = [
            (ident[:], ident_d), (fold[:], fold_d), (causal[:], causal_d), (wqpk_s, w_qpk), (keys_s, keys),
            (win[:, 0, :], w_in[:, 0:DIM]), (win[:, 1, :], w_in[:, DIM:]), (win[:, 2, :], w_in[:, DIM:]),
            (cw[0:DIM, :], conv_w), (cw[DIM:P, :], conv_w), (cb[0:DIM, :], conv_b), (cb[DIM:P, :], conv_b),
            (wbc[:], w_bc), (bbc[:], b_bc), (wlam[:, 0, :], w_lam), (wlam[:, 1, :], w_lam),
            (blam[0:DIM, :], b_lam), (blam[DIM:P, :], b_lam), (wout, w_out), (raw_a, decay),
            (wq[:], w_q), (wo[:], w_o),
        ]

        def ring_free(eng, s, value):
            if not isinstance(value, int) or value > 0:
                eng.wait_ge(s, value)

        def plain(eng):
            eng.sem_inc(passed, 1)

        def norm_of(i, where, c):
            return len(NORMS) * i + NORMS.index((where, c))

        def cols_of(c):
            return slice(c * CH, (c + 1) * CH)

        def tick_batch(b, v):
            return (b, v) if v < SCAN_TICKS else (b + 1, v - SCAN_TICKS)

        def unit_at(v, behind):
            head = v < HEAD_TICKS
            u = v - behind - (0 if head else LAG)
            return u if (0 if head else PAIRS) <= u < (PAIRS if head else UNITS) else None

        block = ctx.enter_context(nc.Block())

        @block.sync
        def _(sync):
            for dst, src in ((dft_s[:], dft), (w18, w_tok)):
                sync.dma_start(dst, src).then_inc(fourier_in, 16)
            for dst, src in loads:
                sync.dma_start(dst, src).then_inc(weights_in, 16)

            def load_half(kind, b, i, half):
                lo = 64 * half
                place = x_place(kind, half)
                if half and kind != "first":
                    sync.wait_ge(wide_filled.sem, wide_filled.after(kind, b, ("tok", 0)))
                elif not half:
                    ring_free(sync, y_summed, UNITS * i)
                sync.dma_start(place[0:CHANNELS, :, :], x[i, :, lo:lo + 64, :]).then_inc(x_in[half], 16)
                if half == 0:
                    sync.dma_start(place[CHANNELS:P, :, :],
                                   x[i, :, STRIDE:STRIDE + 64, :]).then_inc(x_in[0], 16)
                    ring_free(sync, h1_copied, CHUNKS * i)
                    sync.dma_start(h_t[:, TOKENS:LEN], text_t[i]).then_inc(text_in, 16)
                else:
                    last = 64 - STRIDE
                    sync.dma_start(place[CHANNELS:P, 0:last, :],
                                   x[i, :, lo + STRIDE:TIME, :]).then_inc(x_in[1], 16)
                    sync.dma_start(place[CHANNELS:P, last:64, :],
                                   x[i, :, TIME - 1:TIME, :].broadcast_to([CHANNELS, STRIDE, VARS])
                                   ).then_inc(x_in[1], 16)

            def store(b, t):
                sync.wait_ge(out_ready, TILES * b + t + 1 + CREDIT)
                sync.dma_start(out[b, t * P:(t + 1) * P, :], out_s[:]).then_inc(stored, 16)

            sync.sem_inc(stored, 16 * CREDIT)
            for half in range(2):
                load_half("first", 0, 0, half)
            with sync.Fori(0, BATCH - 1) as b:
                for t in range(TILES):
                    if t in (3, 4):
                        load_half("turn", b, b + 1, t - 3)
                    store(b, t)
            for t in range(TILES):
                store(BATCH - 1, t)
            sync.wait_ge(stored, 16 * (TILES * BATCH + CREDIT))

        @block.gpsimd
        def _(pool):
            nc.gpsimd.iota(head_base[:], [[KEYS * KEYS, HEADS]], base=0,
                           channel_multiplier=0).then_inc(pos_ready, 1)
            nc.gpsimd.iota(place[:], [[1, CANDS]], base=0, channel_multiplier=0).then_inc(pos_ready, 1)
            pool.wait_ge(wide_filled.sem, wide_filled.after("first", 0, "wcomb"))
            pool.wait_ge(set_up, SETUP_STEPS)

            def gather(b):
                for t in range(TILES):
                    g = TILES * b + t
                    for h in range(HEADS):
                        pool.wait_ge(row_i_ready, HEADS // 2 * g + h // 2 + 1)
                        pool.wait_ge(rows_summed[h], g + CREDIT)
                        plain(pool)
                        for j in range(TOP):
                            at = h * TOP + j
                            nc.gpsimd.indirect_dma_start(
                                rows[:, h, j, :], None, tables,
                                bass.IndirectOffsetOnAxis(ap=row_i[:, t % 3, at:at + 1], axis=0),
                            ).then_inc(gathered[h], 16)

            with pool.Fori(0, BATCH - 1) as b:
                gather(b)
            gather(BATCH - 1)

        @block.scalar
        def _(act):
            nc.scalar.preload_act_table_set(EXP_AND_LN)
            act.wait_ge(weights_in, 16 * len(loads))
            act.wait_ge(set_up, 2)
            nc.scalar.activation(sp[1], sp[0], ACT.Exp).then_inc(spread, 1)
            act.wait_ge(wide_filled.sem, wide_filled.after("first", 0, "weff"))
            nc.scalar.copy(w_eff[:].rearrange("p k o -> p (k o)"), wide_flat[:, 0:512]).then_inc(wide_drained.sem, 1)
            act.wait_ge(set_up, SETUP_STEPS)

            def keys_copy():
                act.wait_ge(wide_filled.sem, wide_filled.after("first", 0, "wcomb"))
                nc.scalar.copy(wcomb[:], wide_flat[0:DIM, 0:1024]).then_inc(wide_drained.sem, 1)

            def full(kind, b, key):
                act.wait_ge(wide_filled.sem, wide_filled.after(kind, b, key))

            def inverse_root(kind, b, i, where, c):
                n = norm_of(i, where, c)
                full(kind, b, (where, c, "var"))
                nc.scalar.activation(sq, wide[0:DIM, 0, 0:CH], ACT.Ln, bias=ln_eps[0:DIM, :]).then_inc(log_ready, 1)
                act.wait_ge(log_ready, n + 1)
                nc.scalar.activation(sq, sq, ACT.Exp, scale=-0.5).then_inc(inv_ready, 1)

            def tok(kind, b, i, half):
                full(kind, b, ("tok", half))
                if half == 0:
                    ring_free(act, h1_copied, CHUNKS * i)
                dst = h_t[:, 0:TOKENS].rearrange("o (v n) -> o n v", n=PATCHES)[:, 8 * half:8 * half + 8, :]
                src = wide[0:DIM, 0, :].rearrange("o (n v) -> o n v", v=VARS)
                nc.scalar.copy(dst, src).then_inc(wide_drained.sem, 1)

            def front(kind, b, i, c, part):
                if part == 1:
                    inverse_root(kind, b, i, "in", c)
                elif part == 2:
                    full(kind, b, ("in", c, "proj"))
                    nc.scalar.copy(upad[:, TAPS - 1:][:, cols_of(c)], wide[:, 1, 0:CH]).then_inc(u_copied, 1)
                    nc.scalar.activation(gate[:, cols_of(c)], wide[DIM:P, 0, 0:CH], ACT.Gelu
                                         ).then_inc(wide_drained.sem, 1)
                    nc.scalar.preload_act_table_set(EXP_AND_LN)
                elif part == 3:
                    full(kind, b, ("in", c, "gates"))
                    nc.scalar.activation(sig[:, cols_of(c)], wide[:, 1, 0:CH], ACT.Exp, bias=nblam[:], scale=-1.0
                                         ).then_inc(sig_exp, 1)
                    nc.scalar.activation(bc_f[:], wide[:, 0, 0:CH], ACT.Identity, bias=bbc[:]
                                         ).then_inc(wide_drained.sem, 1)
                    act.wait_ge(wide_drained.sem, wide_drained.after(kind, b, ("in", c, "gates")))
                    nc.scalar.copy(bc_t[:, 0, cols_of(c)], bc_f[:]).then_inc(bc_rounded, 1)
                    act.wait_ge(bc_rest, 2 * (CHUNKS * i + c) + 1)
                    nc.scalar.copy(bc_t[:, 1, cols_of(c)], bc_f[:]).then_inc(bc_rounded, 1)

            def tick(i, v):
                u = unit_at(v, 0)
                if u is None:
                    return
                c, p = divmod(u, PAIRS)
                done = UNITS * i + u
                s = sig[:, c * CH:(c + 1) * CH]
                if p == 0:
                    act.wait_ge(sig_step, 2 * (CHUNKS * i + c) + 2)
                ring_free(act, c_ready, done - PICKS + 1)
                nc.scalar.copy(pick[u % PICKS][:], fold[:, 2 * p:2 * p + 2].unsqueeze(2).broadcast_to([P, 2, DIM])
                               ).then_inc(picked, 1)
                ring_free(act, scanned, done - 2)
                nc.scalar.activation(lam_r[u % 3], s, ACT.Exp, scale=coef[:, p:p + 1]).then_inc(lam_ready, 1)
                ring_free(act, scaled, done - 1)
                nc.scalar.activation(z_r[u % 2], s, ACT.Exp, scale=coef2[:, p:p + 1]).then_inc(lam2_ready, 1)
                act.wait_ge(lam2_ready, done + 1)
                nc.scalar.activation(z_r[u % 2], z_r[u % 2], ACT.Ln, bias=one_eps[:], scale=-1.0
                                     ).then_inc(z_log, 1)
                act.wait_ge(z_log, done + 1)
                nc.scalar.activation(z_r[u % 2], z_r[u % 2], ACT.Exp, scale=0.5).then_inc(z_ready, 1)

            def out_of_scan(kind, b, i, c, part):
                if part == 2:
                    inverse_root(kind, b, i, "out", c)
                    act.wait_ge(normed, norm_of(i, "out", c) + 1)
                    nc.scalar.copy(h1_t[:, cols_of(c)], h_t[:, cols_of(c)]).then_inc(h1_copied, 1)

            def query(kind, b, t):
                act.wait_ge(small_filled.sem, small_filled.after(kind, b, ("q", t)))
                nc.scalar.mul(q_t[:].rearrange("p a t -> p (a t)"), small[:], DIM ** -0.5
                              ).then_inc(small_drained.sem, 1)
                act.wait_ge(small_filled.sem, small_filled.after(kind, b, ("res", t)))
                act.wait_ge(out_ready, TILES * b + t - 1 + CREDIT)
                nc.scalar.copy(res[:, t % 3, :], small[:, 0:DIM]).then_inc(small_drained.sem, 1)

            def sim(kind, b, t, g):
                full(kind, b, ("sim", t))
                ring_free(act, rank_step, RANK_STEPS * g)
                nc.scalar.copy(sims[:].rearrange("p g k -> p (g k)"), wide_flat[:, 0:1024]
                               ).then_inc(wide_drained.sem, 1)

            def exponentials(g):
                act.wait_ge(shifted, g + 1)
                ring_free(act, weight_ready, g)
                nc.scalar.activation(expo[:], best[:], ACT.Exp).then_inc(expo_ready, 1)

            def exponential_row(g, t, h):
                act.wait_ge(max_ready, HEADS * g + h + 1)
                nc.scalar.activation(prob[:, 0:(t + 1) * P], wide_flat[:, 0:(t + 1) * P], ACT.Exp,
                                     bias=nmax[:, h:h + 1], accum_out=rsum[:, h:h + 1]
                                     ).then_inc(wide_drained.sem, 1)

            def turned_copy(kind, b, t, h):
                full(kind, b, ("turned", t, h))
                n = (t + 1) * P
                nc.scalar.copy(prob_t[:, 0:n], wide_flat[:, 0:n]).then_inc(wide_drained.sem, 1)

            def weigh(g, t, h):
                act.wait_ge(weight_ready, g + 1)
                act.wait_ge(gathered[h], 16 * TOP * (g + 1))
                for j in range(TOP):
                    last = nc.scalar.mul(rows[:, h, j, :], rows[:, h, j, :], weight[:, t % 3, h, j:j + 1])
                last.then_inc(weighted_odd, 1)

            def row_copy(g, t, h):
                act.wait_ge(rows_summed[h], g + 1 + CREDIT)
                nc.scalar.copy(vals[:, t % TILES, h, :], small[:, DIM:ROW])
                nc.scalar.copy(k_nat[:, h % 2, :], small[:, 0:DIM]).then_inc(small_drained.sem, 1)

            def step(kind, b, t, s, ticks):
                g = TILES * b + t
                attending, summing = attended(t, s), s < HEADS // 2
                tt, pair = attending or (None, 0)
                old, new = (2 * pair, 2 * pair + 1), (2 * s, 2 * s + 1)

                def scan(k):
                    if k < len(ticks):
                        tick(*tick_batch(b, ticks[k]))

                scan(0)
                if attending:
                    exponential_row(TILES * b + tt, tt, old[0])
                    turned_copy(kind, b, tt, old[0])
                scan(1)
                if summing:
                    weigh(g, t, new[1])
                    row_copy(g, t, new[0])
                scan(2)
                if attending:
                    exponential_row(TILES * b + tt, tt, old[1])
                if summing:
                    row_copy(g, t, new[1])
                    act.wait_ge(small_filled.sem, small_filled.after(kind, b, ("keys", t, s)))
                    lo = t % TILES * P
                    nc.scalar.copy(k_t[:, s, lo:lo + P], small[:, 0:P]).then_inc(small_drained.sem, 1)
                for k in range(3, len(ticks)):
                    scan(k)
                if attending:
                    turned_copy(kind, b, tt, old[1])
                if s == 2 and (kind == "turn" or t + 1 < TILES):
                    exponentials(g + 1)

            def finish(g):
                act.wait_ge(o_turned, g + 1)
                nc.scalar.copy(o_t[:].rearrange("p c t -> p (c t)"), attn[:]).then_inc(o_t_ready, 1)

            def turn(kind, b):
                for name, a, n in stages(kind):
                    i = b if kind == "first" or (name, a) in OWN else b + 1
                    if name == "keys":
                        keys_copy()
                    elif name == "tok":
                        tok(kind, b, i, a)
                    elif name == "front":
                        front(kind, b, i, a, n)
                    elif name == "ticks":
                        for v in n:
                            tick(0, v)
                    elif name == "out":
                        out_of_scan(kind, b, i, a, n)
                    elif name == "query":
                        query(kind, b, a)
                    elif name == "sim":
                        sim(kind, b, a, TILES * b + a)
                    elif name == "rank" and n == 3:
                        exponentials(0)
                    elif name == "step":
                        step(kind, b, a, *n)
                    elif name == "finish":
                        finish(TILES * b + a)

            turn("first", 0)
            with act.Fori(0, BATCH - 1) as b:
                turn("turn", b)
            turn("last", BATCH - 1)

        @block.vector
        def _(dve):
            nc.vector.memset(mean_w[:], 1.0 / DIM)
            nc.vector.memset(upad[:, 0:TAPS - 1], 0.0)
            nc.vector.memset(one_eps[:], 1.0 + DECAY_EPS)
            nc.vector.memset(ln_eps[:], LN_EPS)
            dve.wait_ge(weights_in, 16 * len(loads))
            count = [0]

            def step(ins):
                count[0] += 1
                ins.then_inc(set_up, 1)
                dve.wait_ge(set_up, count[0])

            step(nc.vector.tensor_scalar(sp[0], raw_a, -1.0, None, ALU.mult))
            step(nc.vector.tensor_tensor(sp[0], sp[0], raw_a, ALU.min))
            dve.wait_ge(spread, 1)
            step(nc.vector.tensor_scalar(sp[2], sp[1], 2.0, None, ALU.add))
            step(nc.vector.reciprocal(sp[2], sp[2]))
            step(nc.vector.tensor_tensor(sp[1], sp[1], sp[2], ALU.mult))
            step(nc.vector.tensor_tensor(sp[2], sp[1], sp[1], ALU.mult))
            step(nc.vector.tensor_scalar(sp[3], sp[2], 1.0 / SERIES[0], None, ALU.mult))
            for k in SERIES[1:]:
                step(nc.vector.scalar_tensor_tensor(sp[3], sp[3], 1.0 / k, sp[2], ALU.add, ALU.mult))
            step(nc.vector.scalar_tensor_tensor(sp[3], sp[3], 1.0, sp[1], ALU.add, ALU.mult))
            step(nc.vector.tensor_scalar(sp[0], raw_a, 0.0, None, ALU.max))
            step(nc.vector.scalar_tensor_tensor(sp[3], sp[3], 2.0, sp[0], ALU.mult, ALU.add))
            step(nc.vector.tensor_scalar(coef[:], sp[3], -8.0, None, ALU.mult))
            step(nc.vector.tensor_scalar(coef2[:], sp[3], -16.0, None, ALU.mult))
            step(nc.vector.tensor_scalar(nblam[:], blam[:], -1.0, None, ALU.mult))
            assert count[0] == SETUP_STEPS
            dve.wait_ge(pos_ready, 2)

            def full(kind, b, key):
                dve.wait_ge(wide_filled.sem, wide_filled.after(kind, b, key))

            def centre(kind, b, i, where, c):
                full(kind, b, (where, c, "mean"))
                ring_free(dve, normed, norm_of(i, where, c))
                nc.vector.tensor_tensor(xc, h_t[:, cols_of(c)], wide[0:DIM, 0, 0:CH], ALU.subtract
                                        ).then_inc(wide_drained.sem, 1)
                dve.wait_ge(wide_drained.sem, wide_drained.after(kind, b, (where, c, "mean")))
                nc.vector.tensor_tensor(sq, xc, xc, ALU.mult).then_inc(squared, 1)

            def scale(kind, b, i, where, c, dst):
                n = norm_of(i, where, c)
                full(kind, b, (where, c, "var"))
                dve.wait_ge(inv_ready, n + 1)
                nc.vector.tensor_tensor(rr, sq, sq, ALU.mult).then_inc(newton, 1)
                dve.wait_ge(newton, 3 * n + 1)
                nc.vector.scalar_tensor_tensor(rr, wide[0:DIM, 0, 0:CH], LN_EPS, rr, ALU.add, ALU.mult
                                               ).then_inc(wide_drained.sem, 1)
                dve.wait_ge(wide_drained.sem, wide_drained.after(kind, b, (where, c, "var")))
                nc.vector.tensor_scalar(rr, rr, -0.5, 1.5, ALU.mult, ALU.add).then_inc(newton, 1)
                dve.wait_ge(newton, 3 * n + 2)
                nc.vector.tensor_tensor(rr, rr, sq, ALU.mult).then_inc(newton, 1)
                dve.wait_ge(newton, 3 * n + 3)
                nc.vector.tensor_tensor(dst, xc, rr, ALU.mult).then_inc(normed, 1)

            def front(kind, b, i, c, part):
                done = CHUNKS * i + c
                cols = cols_of(c)
                if part == 0:
                    centre(kind, b, i, "in", c)
                elif part == 1:
                    scale(kind, b, i, "in", c, x_c[:, cols])
                elif part == 2:
                    dve.wait_ge(u_copied, done + 1)
                    lo = c * CH
                    nc.vector.tensor_scalar(u_t[:, cols], upad[:, lo:lo + CH], cw[:, 0:1], cb[:, 0:1],
                                            ALU.mult, ALU.add).then_inc(convolved, 1)
                    for k in range(1, TAPS):
                        dve.wait_ge(convolved, TAPS * done + k)
                        nc.vector.scalar_tensor_tensor(u_t[:, cols], upad[:, lo + k:lo + k + CH], cw[:, k:k + 1],
                                                       u_t[:, cols], ALU.mult, ALU.add).then_inc(convolved, 1)
                else:
                    dve.wait_ge(sig_exp, done + 1)
                    nc.vector.tensor_scalar(sig[:, cols], sig[:, cols], 1.0, None, ALU.add).then_inc(sig_step, 1)
                    dve.wait_ge(sig_step, 2 * done + 1)
                    nc.vector.reciprocal(sig[:, cols], sig[:, cols]).then_inc(sig_step, 1)
                    dve.wait_ge(bc_rounded, 2 * done + 1)
                    nc.vector.tensor_tensor(bc_f[:], bc_f[:], bc_t[:, 0, cols], ALU.subtract).then_inc(bc_rest, 1)
                    dve.wait_ge(bc_rounded, 2 * done + 2)
                    nc.vector.tensor_tensor(bc_t[:, 2, cols], bc_f[:], bc_t[:, 1, cols], ALU.subtract
                                            ).then_inc(bc_rest, 1)
                    dve.wait_ge(convolved, TAPS * done + TAPS)
                    plain(dve)

            def tick(i, v):
                u = unit_at(v, 1)
                if u is not None:
                    c = u // PAIRS
                    done = UNITS * i + u
                    dve.wait_ge(b_ready, done + 1)
                    ring_free(dve, scanned, done - 2)
                    nc.vector.tensor_tensor(v_r[u % 3], bwide[:, 0:CH], u_t[:, c * CH:(c + 1) * CH],
                                            ALU.mult).then_inc(bu_ready, 1)
                u = unit_at(v, 4)
                if u is not None:
                    p = u % PAIRS
                    done = UNITS * i + u
                    dve.wait_ge(scanned, done + 1)
                    nc.vector.tensor_copy(carry[:, p:p + 1], hs_r[u % 2][:, CH - 1:CH]).then_inc(carried, 1)
                    dve.wait_ge(c_ready, done + 1)
                    ring_free(dve, y_summed, done - 1)
                    nc.vector.tensor_tensor(cy_r[u % 2], hs_r[u % 2], cwide[:, 0:CH], ALU.mult
                                            ).then_inc(cy_ready, 1)
                u = unit_at(v, 2)
                if u is not None:
                    done = UNITS * i + u
                    dve.wait_ge(bu_ready, done + 1)
                    dve.wait_ge(z_ready, done + 1)
                    nc.vector.tensor_tensor(v_r[u % 3], z_r[u % 2], v_r[u % 3], ALU.mult).then_inc(scaled, 1)
                u = unit_at(v, 3)
                if u is not None:
                    c, p = divmod(u, PAIRS)
                    done = UNITS * i + u
                    dve.wait_ge(scaled, done + 1)
                    dve.wait_ge(lam_ready, done + 1)
                    start = 0.0
                    if c:
                        start = carry[:, p:p + 1]
                        dve.wait_ge(carried, UNITS * i + u - PAIRS + 1)
                    ring_free(dve, cy_ready, done - 1)
                    nc.vector.tensor_tensor_scan(hs_r[u % 2], lam_r[u % 3], v_r[u % 3], start,
                                                 ALU.mult, ALU.add).then_inc(scanned, 1)

            def out_of_scan(kind, b, i, c, part):
                cols = cols_of(c)
                if part == 0:
                    dve.wait_ge(y_summed, UNITS * i + (c + 1) * PAIRS)
                    nc.vector.tensor_tensor(gy, gate[:, cols], ysum[DIM:P, 0:CH], ALU.mult).then_inc(gated, 1)
                    dve.wait_ge(small_filled.sem, small_filled.after(kind, b, ("out", c)))
                    nc.vector.tensor_tensor(h_t[:, cols], h_t[:, cols], small[0:DIM, 0:CH], ALU.add
                                            ).then_inc(small_drained.sem, 1)
                elif part == 1:
                    centre(kind, b, i, "out", c)
                else:
                    scale(kind, b, i, "out", c, xn_t[:, cols])

            def rank(kind, b, t, g, piece):
                first = RANK_STEPS * g + RANK_AT[piece]
                count = [0]

                def after(ins):
                    count[0] += 1
                    ins.then_inc(rank_step, 1)
                    dve.wait_ge(rank_step, first + count[0])
                    plain(dve)

                RANK_PIECES[piece](kind, b, t, g, after)
                assert count[0] == RANK_AT[piece + 1] - RANK_AT[piece], (piece, count)

            groups = range(2 * HEADS)

            def first_eight(kind, b, t, g, after):
                dve.wait_ge(wide_drained.sem, wide_drained.after(kind, b, ("sim", t)))
                plain(dve)
                for q in groups:
                    last = nc.vector.max(top_v[:, q, 0:8], sims[:, q, :])
                after(last)
                for q in groups:
                    nc.vector.max_index(top_i[:, q, 0:8], top_v[:, q, 0:8], sims[:, q, :])
                for q in groups:
                    last = nc.vector.match_replace(sims[:, q, :], top_v[:, q, 0:8], sims[:, q, :], LOWEST)
                after(last)

            def pairs(dst, first, second):
                for a in range(5):
                    m, o = LIMITS[a], PLACES[a]
                    nc.vector.tensor_tensor(dst[:, :, o:o + m], second[:, :, 0:m],
                                            first[:, :, a:a + 1].broadcast_to([P, HEADS, m]), ALU.add)
                o = PLACES[5]
                nc.vector.tensor_tensor(
                    dst[:, :, o:o + 6].rearrange("p h (a c) -> p h a c", c=2),
                    second[:, :, 0:2].unsqueeze(2).broadcast_to([P, HEADS, 3, 2]),
                    first[:, :, 5:8].unsqueeze(3).broadcast_to([P, HEADS, 3, 2]), ALU.add)
                return nc.vector.tensor_tensor(dst[:, :, PLACES[8]:], first[:, :, 8:],
                                               second[:, :, 0:1].broadcast_to([P, HEADS, 8]), ALU.add)

            def next_eight(kind, b, t, g, after):
                for q in groups:
                    last = nc.vector.max(top_v[:, q, 8:16], sims[:, q, :])
                after(last)
                for q in groups:
                    last = nc.vector.max_index(top_i[:, q, 8:16], top_v[:, q, 8:16], sims[:, q, :])
                after(last)
                after(nc.vector.tensor_scalar(idx1[:], top_i[:, HEADS:, :], float(KEYS), None, ALU.mult))
                pairs(cand[:], top_v[:, 0:HEADS, :], top_v[:, HEADS:, :])
                after(pairs(cand_i[:], top_i[:, 0:HEADS, :], idx1[:]))

            def best_pairs(kind, b, t, g, after):
                for h in range(HEADS):
                    last = nc.vector.max(best[:, h, 0:8], cand[:, h, :])
                after(last)
                for h in range(HEADS):
                    nc.vector.max_index(best_at[:, h, 0:8], best[:, h, 0:8], cand[:, h, :])
                for h in range(HEADS):
                    last = nc.vector.match_replace(cand[:, h, :], best[:, h, 0:8], cand[:, h, :], LOWEST)
                after(last)
                for h in range(HEADS):
                    last = nc.vector.max(best[:, h, 8:16], cand[:, h, :])
                after(last)
                for h in range(HEADS):
                    last = nc.vector.max_index(best_at[:, h, 8:16], best[:, h, 8:16], cand[:, h, :])
                after(last)
                ring_free(dve, weight_ready, g)
                after(nc.vector.tensor_copy(zinv[:], best[:, :, 0]))
                nc.vector.tensor_tensor(best[:], best[:], zinv[:].unsqueeze(2).broadcast_to([P, HEADS, TOP]),
                                        ALU.subtract).then_inc(shifted, 1)

            def row_numbers(t, ks, after):
                for k in ks:
                    two = slice(2 * k, 2 * k + 2)
                    shape = [P, 2, TOP, CANDS]
                    after(nc.vector.tensor_tensor(
                        hot[:], best_at[:, two, :].unsqueeze(3).broadcast_to(shape),
                        place[:].unsqueeze(1).unsqueeze(1).broadcast_to(shape), ALU.is_equal))
                    after(nc.vector.tensor_tensor(
                        hot[:], hot[:], cand_i[:, two, :].unsqueeze(2).broadcast_to(shape), ALU.mult))
                    after(nc.vector.tensor_reduce(row_f[:, two, :], hot[:], AX.X, ALU.add))
                    nc.vector.tensor_tensor(row_i[:, t % 3, :].rearrange("p (h j) -> p h j", j=TOP)[:, two, :],
                                            row_f[:, two, :], head_base[:, two].unsqueeze(2)
                                            .broadcast_to([P, 2, TOP]), ALU.add).then_inc(row_i_ready, 1)

            def rows_0(kind, b, t, g, after):
                row_numbers(t, (0,), after)

            def rows_1(kind, b, t, g, after):
                row_numbers(t, (1, 2), after)

            def rows_2(kind, b, t, g, after):
                row_numbers(t, (3,), after)

            def softmax(kind, b, t, g, after):
                dve.wait_ge(expo_ready, g + 1)
                after(nc.vector.tensor_reduce(zsum[:], expo[:], AX.X, ALU.add))
                after(nc.vector.reciprocal(zinv[:], zsum[:]))
                nc.vector.tensor_tensor(weight[:, t % 3, :, :], expo[:],
                                        zinv[:].unsqueeze(2).broadcast_to([P, HEADS, TOP]), ALU.mult
                                        ).then_inc(weight_ready, 1)

            RANK_PIECES = (first_eight, next_eight, best_pairs, rows_0, rows_1, rows_2, softmax)
            RANK_AT = (0, 2, 6, 11, 14, 20, 23, 25)
            assert RANK_AT[-1] == RANK_STEPS

            def step(kind, b, t, s, ticks):
                g = TILES * b + t

                def scan(k):
                    if k < len(ticks):
                        tick(*tick_batch(b, ticks[k]))

                def weigh(h):
                    dve.wait_ge(weight_ready, g + 1)
                    dve.wait_ge(gathered[h], 16 * TOP * (g + 1))
                    nc.vector.tensor_tensor(rows[:, h, :, :], rows[:, h, :, :],
                                            weight[:, t % 3, h, :].unsqueeze(2).broadcast_to([P, TOP, ROW]),
                                            ALU.mult).then_inc(weighted_even, 1)

                def halve(h):
                    dve.wait_ge((weighted_even, weighted_odd)[h % 2], HEADS // 2 * g + h // 2 + 1)
                    nc.vector.tensor_tensor(rows[:, h, 0:FOLDED, :], rows[:, h, 0:FOLDED, :],
                                            rows[:, h, FOLDED:TOP, :], ALU.add).then_inc(halved, 1)

                ranking = s < 4 and (kind == "turn" or t + 1 < TILES)
                attending = attended(t, s)
                tt, pair = attending or (None, 0)
                scan(0)
                if ranking:
                    rank(kind, b, t + 1, g + 1, 2 * s)
                if attending:
                    row_max(kind, b, tt, 2 * pair)
                scan(1)
                if s < HEADS // 2:
                    weigh(2 * s)
                    halve(2 * s)
                if s == 1 and t:
                    close(g - 1, t - 1)
                scan(2)
                if s < HEADS // 2:
                    halve(2 * s + 1)
                if attending:
                    row_max(kind, b, tt, 2 * pair + 1)
                for k in range(3, len(ticks)):
                    scan(k)
                if ranking and s < 3:
                    rank(kind, b, t + 1, g + 1, 2 * s + 1)

            def row_max(kind, b, t, h):
                full(kind, b, ("score", t, h))
                nc.vector.tensor_reduce(nmax[:, h:h + 1], wide_flat[:, 0:(t + 1) * P], AX.X, ALU.max,
                                        negate=True).then_inc(max_ready, 1)

            def finish(g):
                dve.wait_ge(o_filled, g + 1)
                dve.wait_ge(o_normed, g + CREDIT)
                nc.vector.reciprocal(rinv[:], rsum[:]).then_inc(o_inv, 1)
                dve.wait_ge(o_inv, g + 1)
                nc.vector.tensor_tensor(o_n[:], attn[:].rearrange("p (h d) -> p h d", d=DIM),
                                        rinv[:].unsqueeze(2).broadcast_to([P, HEADS, DIM]), ALU.mult
                                        ).then_inc(o_normed, 1)

            def close(g, t):
                dve.wait_ge(fin_filled, g + 1)
                dve.wait_ge(stored, 16 * (g + CREDIT))
                nc.vector.tensor_tensor(out_s[:], res[:, t % 3, :], attn[:, 0:DIM], ALU.add).then_inc(out_ready, 1)

            def turn(kind, b):
                for name, a, n in stages(kind):
                    i = b if kind == "first" or (name, a) in OWN else b + 1
                    if name == "front":
                        front(kind, b, i, a, n)
                    elif name == "ticks":
                        for v in n:
                            tick(0, v)
                    elif name == "out":
                        out_of_scan(kind, b, i, a, n)
                    elif name == "rank":
                        for piece in (2 * n, 2 * n + 1)[:1 + (n < 3)]:
                            rank(kind, b, a, a, piece)
                    elif name == "step":
                        step(kind, b, a, *n)
                    elif name == "finish":
                        finish(TILES * b + a)
                    elif name == "close":
                        close(TILES * b + a, a)

            dve.sem_inc(o_normed, CREDIT)
            dve.sem_inc(out_ready, CREDIT)
            turn("first", 0)
            with dve.Fori(0, BATCH - 1) as b:
                turn("turn", b)
            turn("last", BATCH - 1)

        @block.tensor
        def _(pe):
            pe.wait_ge(fourier_in, 16 * 2)
            for o in range(DIM):
                for late in range(2):
                    dst = wide_flat[CHANNELS * late:CHANNELS * late + CHANNELS, 0:512]
                    mm = nc.tensor.matmul(dst.rearrange("p (k o) -> p k o", o=DIM)[:, :, o], w18[:, o, :],
                                          dft_s[:, STRIDE * late:STRIDE * late + STRIDE], start=True, stop=True)
            mm.then_inc(wide_filled.sem, 1)
            pe.wait_ge(weights_in, 16 * len(loads))
            pe.wait_ge(set_up, 1)

            def free_wide(kind, b, key):
                pe.wait_ge(wide_drained.sem, wide_drained.before(kind, b, key))
                plain(pe)

            def fold_keys():
                free_wide("first", 0, "wcomb")
                for q in range(2 * HEADS):
                    mm = nc.tensor.matmul(wide_flat[0:DIM, q * KEYS:(q + 1) * KEYS], wqpk_s[:, q, :],
                                          keys_s[:, q, :], start=True, stop=True)
                mm.then_inc(wide_filled.sem, 1)

            def free_small(kind, b, key):
                pe.wait_ge(small_drained.sem, small_drained.before(kind, b, key))
                plain(pe)

            def project(bank, parts, lhs, rhs):
                return nc.tensor.matmul(wide[parts, bank, 0:CH], lhs, rhs, start=True, stop=True)

            def mean_of(kind, b, i, where, c):
                free_wide(kind, b, (where, c, "mean"))
                project(0, slice(0, DIM), mean_w[:], h_t[:, cols_of(c)]).then_inc(wide_filled.sem, 1)

            def variance_of(kind, b, i, where, c):
                pe.wait_ge(squared, norm_of(i, where, c) + 1)
                free_wide(kind, b, (where, c, "var"))
                project(0, slice(0, DIM), mean_w[:], sq).then_inc(wide_filled.sem, 1)

            def tok(kind, b, i, half):
                pe.wait_ge(x_in[half], (32 + 16 * half) * (i + 1))
                free_wide(kind, b, ("tok", half))
                for k in range(STRIDE):
                    mm = nc.tensor.matmul(wide[0:DIM, 0, :], w_eff[:, k, :], x_place(kind, half)[:, k:64:STRIDE, :],
                                          start=(k == 0), stop=(k == STRIDE - 1))
                mm.then_inc(wide_filled.sem, 1)

            def front(kind, b, i, c, part):
                cols = cols_of(c)
                if part == 0:
                    if c == CHUNKS - 1:
                        pe.wait_ge(text_in, 16 * (i + 1))
                    mean_of(kind, b, i, "in", c)
                elif part == 1:
                    variance_of(kind, b, i, "in", c)
                elif part == 2:
                    pe.wait_ge(normed, norm_of(i, "in", c) + 1)
                    free_wide(kind, b, ("in", c, "proj"))
                    project(0, slice(DIM, P), win[:, 0, :], x_c[:, cols])
                    project(1, slice(0, P), win[:, 1:3, :], x_c[:, cols]).then_inc(wide_filled.sem, 1)
                else:
                    pe.wait_ge(convolved, TAPS * (CHUNKS * i + c) + TAPS)
                    free_wide(kind, b, ("in", c, "gates"))
                    project(0, slice(0, P), wbc[:], u_t[0:DIM, cols])
                    project(1, slice(0, P), wlam[:], u_t[0:DIM, cols]).then_inc(wide_filled.sem, 1)

            def spread_state(dst, rows, u, c):
                for part in range(PARTS):
                    mm = nc.tensor.matmul(dst[:, 0:CH], pick[u % PICKS][rows, :, :].rearrange("p a b -> p (a b)"),
                                          bc_t[rows, part, c * CH:(c + 1) * CH], start=(part == 0),
                                          stop=(part == PARTS - 1))
                return mm

            def tick(i, v):
                u = unit_at(v, 0)
                if u is not None:
                    ring_free(pe, bu_ready, UNITS * i + u)
                    pe.wait_ge(picked, UNITS * i + u + 1)
                    if u % PAIRS == 0:
                        pe.wait_ge(bc_rest, 2 * (CHUNKS * i + u // PAIRS) + 2)
                    plain(pe)
                    spread_state(bwide, slice(0, STATE), u, u // PAIRS).then_inc(b_ready, 1)
                u = unit_at(v, 3)
                if u is not None:
                    ring_free(pe, cy_ready, UNITS * i + u)
                    plain(pe)
                    spread_state(cwide, slice(STATE, P), u, u // PAIRS).then_inc(c_ready, 1)
                u = unit_at(v, LAG)
                if u is not None:
                    c, p = divmod(u, PAIRS)
                    pe.wait_ge(cy_ready, UNITS * i + u + 1)
                    if p == 0:
                        ring_free(pe, gated, CHUNKS * i + c)
                    nc.tensor.matmul(ysum[DIM:P, 0:CH], fold[:], cy_r[u % 2], start=(p == 0),
                                     stop=(p == PAIRS - 1)).then_inc(y_summed, 1)

            def out_of_scan(kind, b, i, c, part):
                if part == 0:
                    pe.wait_ge(gated, CHUNKS * i + c + 1)
                    free_small(kind, b, ("out", c))
                    nc.tensor.matmul(small[0:DIM, 0:CH], wout, gy, start=True, stop=True
                                     ).then_inc(small_filled.sem, 1)
                elif part == 1:
                    pe.wait_ge(small_drained.sem, small_drained.after(kind, b, ("out", c)))
                    mean_of(kind, b, i, "out", c)
                else:
                    variance_of(kind, b, i, "out", c)

            def query(kind, b, t):
                pe.wait_ge(normed, norm_of(b + t // TILES, "out", t % TILES // 3) + 1)
                free_small(kind, b, ("q", t))
                tile = slice(t % TILES * P, (t % TILES + 1) * P)
                for hp in range(HEADS // 2):
                    mm = nc.tensor.matmul(small[:, hp * P:(hp + 1) * P], wq[:, hp * P:(hp + 1) * P],
                                          xn_t[:, tile], start=True, stop=True)
                mm.then_inc(small_filled.sem, 1)
                pe.wait_ge(h1_copied, CHUNKS * b + t // 3 + 1)
                free_small(kind, b, ("res", t))
                nc.tensor.transpose(small[:, 0:DIM], h1_t[:, tile], ident[DIM:P, DIM:P]
                                    ).then_inc(small_filled.sem, 1)

            def sim(kind, b, t, i):
                pe.wait_ge(normed, norm_of(i, "out", t % TILES // 3) + 1)
                free_wide(kind, b, ("sim", t))
                for n in range(2):
                    mm = nc.tensor.matmul(wide[:, n, :], xn_t[:, (t % TILES) * P:(t % TILES + 1) * P],
                                          wcomb[:, n * 512:(n + 1) * 512], start=True, stop=True)
                mm.then_inc(wide_filled.sem, 1)

            def scores(kind, b, t, h):
                hp, half = h // 2, DIM * (h % 2)
                free_wide(kind, b, ("score", t, h))
                n = (t + 1) * P
                for lo in range(0, n, 512):
                    hi = min(lo + 512, n)
                    mm = nc.tensor.matmul(wide_flat[:, lo:hi], q_t[half:half + DIM, hp, :],
                                          k_t[half:half + DIM, hp, lo:hi], start=True, stop=(hi < n))
                nc.tensor.matmul(wide_flat[:, n - P:n], ident[:], causal[:], start=False, stop=True
                                 ).then_inc(wide_filled.sem, 1)

            def turned(kind, b, t, h):
                free_wide(kind, b, ("turned", t, h))
                for j in range(t + 1):
                    mm = nc.tensor.transpose(wide_flat[:, j * P:(j + 1) * P], prob[:, j * P:(j + 1) * P], ident[:])
                mm.then_inc(wide_filled.sem, 1)

            def attend(kind, b, t, h):
                pe.wait_ge(wide_drained.sem, wide_drained.after(kind, b, ("turned", t, h)))
                if h == 0:
                    pe.wait_ge(out_ready, TILES * b + t + CREDIT)
                for j in range(t + 1):
                    mm = nc.tensor.matmul(attn[:, h * DIM:(h + 1) * DIM], prob_t[:, j * P:(j + 1) * P],
                                          vals[:, j, h, :], start=(j == 0), stop=(j == t))
                if h == HEADS - 1:
                    mm.then_inc(o_filled, 1)

            def row_sum(kind, b, t, h):
                pe.wait_ge(halved, HEADS * (TILES * b + t) + h + 1)
                free_small(kind, b, ("kv", t, h))
                for j in range(FOLDED):
                    mm = nc.tensor.matmul(small[:, 0:ROW], ident[:], rows[:, h, j, :], start=(j == 0),
                                          stop=(j == FOLDED - 1))
                mm.then_inc(rows_summed[h], 1)

            def step(kind, b, t, s, ticks):
                attending, summing = attended(t, s), s < HEADS // 2
                tt, pair = attending or (None, 0)
                old, new = (2 * pair, 2 * pair + 1), (2 * s, 2 * s + 1)

                def scan(k):
                    if k < len(ticks):
                        tick(*tick_batch(b, ticks[k]))

                if attending:
                    pe.wait_ge(small_drained.sem, small_drained.after(kind, b, ("keys", tt, pair) if tt or pair else None))
                    scores(kind, b, tt, old[0])
                scan(0)
                if attending:
                    turned(kind, b, tt, old[0])
                scan(1)
                if summing:
                    row_sum(kind, b, t, new[0])
                if attending:
                    scores(kind, b, tt, old[1])
                scan(2)
                if attending:
                    attend(kind, b, tt, old[0])
                if summing:
                    row_sum(kind, b, t, new[1])
                    free_small(kind, b, ("keys", t, s))
                    nc.tensor.transpose(small[:, 0:P], k_nat[:].rearrange("p h d -> p (h d)"), ident[:]
                                        ).then_inc(small_filled.sem, 1)
                if attending:
                    turned(kind, b, tt, old[1])
                for k in range(3, len(ticks)):
                    scan(k)
                if attending:
                    attend(kind, b, tt, old[1])

            def finish(g):
                pe.wait_ge(o_normed, g + 1 + CREDIT)
                for c in range(HEADS // 2):
                    mm = nc.tensor.transpose(attn[:, c * P:(c + 1) * P],
                                             o_n[:].rearrange("p h d -> p (h d)")[:, c * P:(c + 1) * P], ident[:])
                mm.then_inc(o_turned, 1)
                pe.wait_ge(o_t_ready, g + 1)
                for c in range(HEADS // 2):
                    mm = nc.tensor.matmul(attn[:, 0:DIM], o_t[:, c, :], wo[:, c, :], start=(c == 0),
                                          stop=(c == HEADS // 2 - 1))
                mm.then_inc(fin_filled, 1)

            def turn(kind, b):
                for name, a, n in stages(kind):
                    i = b if kind == "first" or (name, a) in OWN else b + 1
                    if name == "keys":
                        fold_keys()
                    elif name == "tok":
                        tok(kind, b, i, a)
                    elif name == "front":
                        front(kind, b, i, a, n)
                    elif name == "ticks":
                        for v in n:
                            tick(0, v)
                    elif name == "out":
                        out_of_scan(kind, b, i, a, n)
                    elif name == "query":
                        query(kind, b, a)
                    elif name == "sim":
                        sim(kind, b, a, b + a // TILES)
                    elif name == "step":
                        step(kind, b, a, *n)
                    elif name == "finish":
                        finish(TILES * b + a)

            for h in range(HEADS):
                pe.sem_inc(rows_summed[h], CREDIT)
            turn("first", 0)
            with pe.Fori(0, BATCH - 1) as b:
                turn("turn", b)
            turn("last", BATCH - 1)


EXP_AND_LN = "natural_log_exp_and_others"
SERIES = (17, 15, 13, 11, 9, 7, 5, 3)
SETUP_STEPS = 12 + len(SERIES)


def dft_table():
    angle = 2 * np.pi * np.arange(FREQS)[:, None] * np.arange(PATCH)[None, :] / PATCH
    return (np.concatenate([np.cos(angle), -np.sin(angle)]) / np.sqrt(PATCH)).astype(np.float32)


def kernel(**inputs):
    import concourse.bacc as bacc
    from concourse.bass_utils import run_bass_kernel_spmd

    a = {k: np.asarray(v) for k, v in inputs.items()}
    col = lambda v: v.reshape(-1, 1)
    arrays = {
        "x": a["x"],
        "text": a["txt"],
        "text_t": a["txt"].transpose(0, 2, 1),
        "w_tok": a["L0_tok_W"].reshape(DIM, 2 * FREQS, CHANNELS).transpose(1, 0, 2),
        "dft": dft_table(),
        "w_in": a["L0_attn_W_in"].T,
        "conv_w": a["L0_attn_conv_w"].reshape(DIM, TAPS),
        "conv_b": col(a["L0_attn_conv_b"]),
        "w_bc": a["L0_attn_W_bc"].T,
        "b_bc": col(a["L0_attn_b_bc"]),
        "w_lam": a["L0_attn_W_lam"].T,
        "b_lam": col(a["L0_attn_b_lam"]),
        "decay": a["L0_attn_A"].reshape(PAIRS, 2, DIM).transpose(1, 2, 0).reshape(P, PAIRS),
        "w_out": a["L0_attn_W_out"].T,
        "w_qpk": a["L0_ffn_Wq_pk"].reshape(DIM, 2 * HEADS, KEYDIM).transpose(2, 1, 0),
        "keys": a["L0_ffn_pk_keys"].transpose(3, 0, 2, 1).reshape(KEYDIM, 2 * HEADS, KEYS),
        "w_q": a["L0_ffn_Wq"],
        "tables": np.concatenate([a["L0_ffn_keys_table"], a["L0_ffn_values_table"]], axis=1),
        "w_o": a["L0_ffn_Wo"].reshape(HEADS * DIM // P, P, DIM).transpose(1, 0, 2),
        "ident_d": np.eye(P, dtype=np.float32),
        "fold_d": np.tile(np.eye(DIM, dtype=np.float32), (2, 1)),
        "causal_d": np.triu(np.full((P, P), MASKED, np.float32), 1),
    }
    nc = bacc.Bacc("TRN2", target_bir_lowering=False, num_devices=1)
    arrays = {f"in_{k}": np.ascontiguousarray(v) for k, v in arrays.items()}
    args = {k[3:]: nc.dram_tensor(k, v.shape, mybir.dt.from_np(v.dtype), kind="ExternalInput").ap()
            for k, v in arrays.items()}
    args["out"] = nc.dram_tensor("out", (BATCH, LEN, DIM), F32, kind="ExternalOutput").ap()
    program(nc, **args)
    r = run_bass_kernel_spmd(nc, [arrays], core_ids=[0])
    return r.results[0]["out"]
```
